# Optimizing a Trainium2 kernel written in Bass

```python
import numpy as np
import jax
import jax.numpy as jnp

def _softmax(x, axis=-1):
    return jax.nn.softmax(x, axis=axis)

def _gelu(x):
    return jax.nn.gelu(x, approximate=True)

def _silu(x):
    return jax.nn.silu(x)

def _sigmoid(x):
    return jax.nn.sigmoid(x)

def _layernorm(x, axis=-1, eps=1e-05):
    m = jnp.mean(x, axis=axis, keepdims=True)
    v = jnp.var(x, axis=axis, keepdims=True)
    return (x - m) / jnp.sqrt(v + eps)

def _scatter_add(tgt, idx, src, axis=0):
    return tgt.at[idx].add(src)

def _segment_sum(src, seg, n):
    return jax.ops.segment_sum(src, seg, n)
kernel_name = 'mk_adj_ffn_d1_adj_r2_c6b4ce'

def setup_inputs(seed: int=0):
    np.random.seed(seed)
    _w = jnp.asarray

    def _rec_inputs():
        import jax
        import jax.numpy as jnp
        _gk = jax.random.key(seed)
        x = -0.0002928 + 1 * jax.random.normal(jax.random.fold_in(_gk, 1), (32, 256, 128), jnp.float32)
        _a = jax.random.bernoulli(jax.random.fold_in(_gk, 2), 0.03125, (32, 256, 256))
        _a = jnp.logical_or(_a, jnp.swapaxes(_a, -1, -2))
        _a = jnp.logical_or(_a, jnp.eye(256, dtype=bool))
        _af = _a.astype(jnp.float32)
        adj = _af
        return (x, adj)
    x, adj = _rec_inputs()

    def _L0_gnn_setup():
        import jax, jax.numpy as jnp
        import numpy as np
        B, N, D_IN, D_OUT = (16, 512, 128, 128)
        NEG_INF = -9000000000000000.0
        LRELU_SLOPE = 0.2
        key = jax.random.key(seed)
        k1, k2, k3, k4 = jax.random.split(key, 4)
        x = jax.random.normal(k1, (B, N, D_IN), dtype=jnp.float32)
        adj_matrix = jax.random.randint(k2, (B, N, N), 0, 2).astype(jnp.float32)
        w_lim = float(np.sqrt(6.0 / (D_IN + D_OUT)))
        a_lim = float(np.sqrt(6.0 / (2 * D_OUT + 1)))
        W = jax.random.uniform(k3, (D_IN, D_OUT), minval=-w_lim, maxval=w_lim, dtype=jnp.float32)
        a = jax.random.uniform(k4, (2 * D_OUT, 1), minval=-a_lim, maxval=a_lim, dtype=jnp.float32)
        return {'x': x, 'adj_matrix': adj_matrix, 'W': W, 'a': a}
    _L0_gnn_all = _L0_gnn_setup()
    _L0_gnn_in = {k: v for k, v in _L0_gnn_all.items() if k in ('W', 'a')}
    del _L0_gnn_all

    def _L0_ffn_setup():
        import jax, jax.numpy as jnp
        import numpy as np
        TOP_K = 2
        key = jax.random.key(seed)
        ks = jax.random.split(key, 4)
        B, L, D, H, E = (8, 2048, 128, 512, 8)
        s = 0.02
        return {'x': jax.random.normal(ks[0], (B, L, D), jnp.float32), 'Wg': jax.random.normal(ks[1], (D, E), jnp.float32) * s, 'bg': jnp.zeros((E,), jnp.float32), 'W1': jax.random.normal(ks[2], (E, D, H), jnp.float32) * s, 'b1': jnp.zeros((E, H), jnp.float32), 'W2': jax.random.normal(ks[3], (E, H, D), jnp.float32) * s, 'b2': jnp.zeros((E, D), jnp.float32)}
    _L0_ffn_all = _L0_ffn_setup()
    _L0_ffn_in = {k: v for k, v in _L0_ffn_all.items() if k in ('Wg', 'bg', 'W1', 'b1', 'W2', 'b2')}
    del _L0_ffn_all
    return {'x': x, 'adj': adj, 'L0_gnn_W': _L0_gnn_in['W'], 'L0_gnn_a': _L0_gnn_in['a'], 'L0_ffn_Wg': _L0_ffn_in['Wg'], 'L0_ffn_bg': _L0_ffn_in['bg'], 'L0_ffn_W1': _L0_ffn_in['W1'], 'L0_ffn_b1': _L0_ffn_in['b1'], 'L0_ffn_W2': _L0_ffn_in['W2'], 'L0_ffn_b2': _L0_ffn_in['b2']}

def reference(x, adj, L0_gnn_W, L0_gnn_a, L0_ffn_Wg, L0_ffn_bg, L0_ffn_W1, L0_ffn_b1, L0_ffn_W2, L0_ffn_b2):
    import jax
    import jax.numpy as jnp

    def _L0_gnn_ref(x, adj_matrix, W, a):
        import jax, jax.numpy as jnp
        import numpy as np
        B, N, D_IN, D_OUT = (16, 512, 128, 128)
        NEG_INF = -9000000000000000.0
        LRELU_SLOPE = 0.2
        h = jnp.einsum('bni,io->bno', x, W)
        d = h.shape[-1]
        a1 = a[:d, 0]
        a2 = a[d:, 0]
        src = h @ a1
        dst = h @ a2
        e = src[:, :, None] + dst[:, None, :]
        e = jnp.where(e >= 0, e, LRELU_SLOPE * e)
        masked_e = jnp.where(adj_matrix > 0, e, NEG_INF)
        attention = jax.nn.softmax(masked_e, axis=2)
        h_out = jnp.einsum('bij,bjd->bid', attention, h)
        return h_out

    def _L0_ffn_ref(x, Wg, bg, W1, b1, W2, b2):
        import jax, jax.numpy as jnp
        import numpy as np
        TOP_K = 2
        B, L, D = x.shape
        E = W1.shape[0]
        xf = x.reshape(-1, D)
        gate_logits = xf @ Wg + bg
        top_w, top_i = jax.lax.top_k(gate_logits, TOP_K)
        top_w = jax.nn.softmax(top_w, axis=-1)
        w_dense = jnp.sum(jax.nn.one_hot(top_i, E, dtype=xf.dtype) * top_w[..., None], axis=1)
        out = jnp.zeros_like(xf)
        for e in range(E):
            h = jax.nn.gelu(xf @ W1[e] + b1[e], approximate=False)
            out = out + w_dense[:, e:e + 1] * (h @ W2[e] + b2[e])
        return out.reshape(B, L, D)
    x = x + _L0_gnn_ref(_layernorm(x, axis=-1), adj, L0_gnn_W, L0_gnn_a)
    x = x + _L0_ffn_ref(_layernorm(x, axis=-1), L0_ffn_Wg, L0_ffn_bg, L0_ffn_W1, L0_ffn_b1, L0_ffn_W2, L0_ffn_b2)
    return x

_drawn_inputs = setup_inputs


def setup_inputs(seed=0):
    import zlib

    import numpy as np

    out = dict(_drawn_inputs(seed))
    spreads = {'L0_ffn_bg': (0.0, 0.1), 'L0_ffn_b1': (0.0, 0.494), 'L0_ffn_b2': (0.0, 0.1)}
    factors = {}
    for name, (base, spread) in spreads.items():
        noise = np.random.default_rng([zlib.crc32(name.encode()), seed]).standard_normal(out[name].shape)
        drawn = base * np.exp(spread * noise) if base else spread * noise
        out[name] = jnp.asarray(drawn.astype(out[name].dtype))
    for name, factor in factors.items():
        out[name] = (out[name] * factor).astype(out[name].dtype)
    return out
```

```python
from contextlib import ExitStack

import concourse.bass as bass
from concourse import mybir

F32 = mybir.dt.float32
F32R = mybir.dt.float32r
BF16 = mybir.dt.bfloat16
I32 = mybir.dt.int32
U32 = mybir.dt.uint32
ALU = mybir.AluOpType
ACT = mybir.ActivationFunctionType
AX = mybir.AxisListType

P = 128
G, N, D = 32, 256, 128
T = N // P
E, H, K = 8, 512, 2
C = H // P
TOK = G * N
TILES = TOK // P
ROW = D + 2
STRIDE = TOK + P
SLOTS = TOK * K // P + E
PAD_ROWS = (E) * P
XS_ROWS = E * STRIDE + PAD_ROWS
SKIP = TOK * K
NEG = -9000000000000000.0
SLOPE = 0.2
EPS = 1e-5
RING = 8
CH = 8
NCH = TILES // CH

SEMAPHORES = """
    consts_made ident_zero weights_in ffn_weights_in wt_ps wt_sb wa_ps wa_sb wrep_ready
    ln1_stats ln1_mv ln1_log ln1_root ln1_n1 ln1_n2 ln1_rstd xhat_ready
    xhat_t_ps xhat_t_sb h_ps dst_ps h_sb dst_sb relu_sb
    mask_ready e_sum e_max negmax_ready p_ready rinv_ready p_t_ps p_t_sb attn_ps
    x1_ready ln2_stats ln2_mv ln2_log ln2_root ln2_n1 ln2_n2 ln2_rstd rows_ready
    xn_t_ps xn_t_sb logits_ps logits_sb top_ready index_ready picks_ready gap_ready gap_exp
    gate_den gate_first gates_ready onehot_ready sel_ready count_ps pos_ready posmask_ready
    slots_ready base_ready dest_ready dest_moved base_init dest_init
    w1_hi w2_hi w1_lo w2_lo
    cnt_ready over_ready ntile_ready ntri_ready cumend_ready comp_ready eid_ready span_ready
    spanmul_ready rowsum_ready tab_f tab_ready pads_done dummy_done
    xt_ps xt_hi xt_lo up_ps biased gelu_done gt_ps gt_hi gt_lo down_ps y_half y_full y_scaled
    first_add second_add stored passed_pool passed_dve
""".split()


def build(nc, x, adj, W, a, Wg, bg, W1, b1, W2, b2, out):
    xs = nc.dram_tensor("routed_rows", (XS_ROWS, ROW), F32, kind="Internal").ap()
    ytok = nc.dram_tensor("expert_out", (K * TOK, D), F32, kind="Internal").ap()
    x_tiles = x.rearrange("g (t p) d -> p (g t) d", p=P)
    out_tiles = out.rearrange("g (t p) d -> p (g t) d", p=P)
    adj_tiles = adj.rearrange("g (t p) j -> g p t j", p=P)
    y_tiles = ytok.rearrange("(k n p) d -> k p n d", k=K, p=P)

    with ExitStack() as ctx:
        def sb(name, shape, dt=F32):
            return ctx.enter_context(nc.sbuf_tensor(name, shape, dt))

        s = {n: ctx.enter_context(nc.semaphore(n)) for n in SEMAPHORES}
        graph_in = [ctx.enter_context(nc.semaphore(f"graph_in{i}")) for i in range(2)]
        rows_sent = [ctx.enter_context(nc.semaphore(f"rows_sent{i}")) for i in range(2)]
        tile_in = [ctx.enter_context(nc.semaphore(f"tile_in{i}")) for i in range(RING)]
        tile_out = [ctx.enter_context(nc.semaphore(f"tile_out{i}")) for i in range(RING)]
        y_in = [ctx.enter_context(nc.semaphore(f"y_in{i}")) for i in range(4)]

        bank = [ctx.enter_context(nc.psum_tensor(f"bank{i}", [P, 512], F32)) for i in range(8)]

        X = sb("X", [P, TILES + 4, D])
        ident = sb("ident", [P, P])
        tri = sb("tri", [P, P], BF16)
        ones = sb("ones", [P, P], BF16)
        iota_e = sb("iota_e", [P, E])
        Waug = sb("Waug", [P, D + 2])
        Wsb = sb("Wsb", [P, D])
        WT = sb("WT", [P, P])
        a_sb = sb("a_sb", [P, 2])
        wa2 = sb("wa2", [P, P])
        Wg_sb = sb("Wg_sb", [P, E])
        bg_rep = sb("bg_rep", [P, E])
        b1_rep = sb("b1_rep", [P, E, H])
        b2_rep = sb("b2_rep", [P, E, D])
        Wstage = sb("Wstage", [P, 2, E * H])
        W1hi = sb("W1hi", [P, E * H], F32R)
        W1lo = sb("W1lo", [P, E * H], F32R)
        W2hl = sb("W2hl", [P, E * C, 2, D], F32R)
        W1s = Wstage[:, 0, :]
        W2s = Wstage[:, 1, :].rearrange("p (b d) -> p b d", d=D)

        adj_sb = sb("adj_sb", [P, 2, T, N])
        st1 = sb("st1", [P, 2, T, 6])
        mv1 = sb("mv1", [P, 2, T, 2])
        rt1 = sb("rt1", [P, 2, 4, T])
        xhat = sb("xhat", [P, 2, T, D])
        xhatT = sb("xhatT", [P, 2, N])
        h_sb = sb("h_sb", [P, 2, T, D + 2])
        dst_sb = sb("dst_sb", [P, 2, N])
        relu_sb = sb("relu_sb", [P, 2, T, N])
        mask = sb("mask", [P, 2, T, N])
        e_sb = sb("e_sb", [P, 2, T, N])
        emax = sb("emax", [P, 2, T])
        nmax = sb("nmax", [P, 2, T])
        p_sb = sb("p_sb", [P, 2, T, N])
        psums = sb("psums", [P, 2, T])
        rinv = sb("rinv", [P, 2, T])
        pT = sb("pT", [P, 2, T, N])
        st2 = sb("st2", [P, 2, T, 6])
        mv2 = sb("mv2", [P, 2, T, 2])
        rt2 = sb("rt2", [P, 2, 4, T])
        rows = sb("rows", [P, 2, T, K, ROW])
        xnT = sb("xnT", [P, 2, N])
        lg = sb("lg", [P, 2, T, E])
        top = sb("top", [P, 2, T, 8])
        topi = sb("topi", [P, 2, T, 8], U32)
        pick = sb("pick", [P, 2, T, K])
        gap = sb("gap", [P, 2, 4, T])
        hot = sb("hot", [P, 2, T, K, E])
        sel = sb("sel", [P, 2, T, E], BF16)
        pos = sb("pos", [P, 2, T, E])
        posm = sb("posm", [P, 2, T, K, E])
        slot = sb("slot", [P, 2, T, K], I32)
        base = sb("base", [P, E])
        base0 = sb("base0", [P, E])
        dest = sb("dest", [P, T, K])
        eps_t = sb("eps_t", [P, 1])

        cnt = sb("cnt", [1, E])
        edge = sb("edge", [1, TILES])
        ntile = sb("ntile", [1, E])
        low8 = sb("low8", [1, E, E])
        ntri = sb("ntri", [1, E, E])
        cumend = sb("cumend", [1, E])
        tile_no = sb("tile_no", [1, SLOTS])
        eid = sb("eid", [1, SLOTS])
        span = sb("span", [1, E])
        rowsum = sb("rowsum", [1, SLOTS])
        row0 = sb("row0", [1, SLOTS])
        eid_i = sb("eid_i", [1, SLOTS + 8], I32)
        row_i = sb("row_i", [1, SLOTS + 8], I32)
        base_i = sb("base_i", [1, E], I32)
        pad_rows = sb("pad_rows", [P, ROW])

        spare = Wstage[:].rearrange("p k n -> p (k n)")
        taken = [0]

        def part(*shape):
            n = 1
            for d in shape:
                n *= d
            taken[0] += n
            names = "abc"[:len(shape)]
            return spare[:, taken[0] - n:taken[0]].rearrange(
                f"p ({' '.join(names)}) -> p {' '.join(names)}", **dict(zip(names, shape)))

        xt = part(RING, ROW)
        xTh = sb("xTh", [P, 2, P], F32R)
        xTl = sb("xTl", [P, 2, P], F32R)
        hb = part(2, H)
        g_sb = part(2, H)
        gTh = sb("gTh", [P, 2, H], F32R)
        gTl = sb("gTl", [P, 2, H], F32R)
        ya = part(2, D)
        yb = part(2, D)
        ys = part(RING, D)
        comp = part(SLOTS, E)[0:1]
        compm = part(SLOTS, E)[0:1]
        over = part(E, TILES)[0:1]

        def ready(eng, name, g):
            eng.wait_ge(s[name], g + 1)

        def freed(eng, name, g, depth=2):
            if not isinstance(g, int) or g >= depth:
                eng.wait_ge(s[name], g + 1 - depth)

        def alone(eng):
            eng.sem_inc(s["passed_pool" if eng is nc.gpsimd else "passed_dve"], 1)

        def steps_of(eng, start, count, unroll, lag, step):
            for i in range(start):
                step(i, i % unroll)
            with eng.Fori(start, count - unroll + 1, unroll) as i0:
                for j in range(unroll):
                    step(i0 + j, j)
            for i in range(count, count + lag):
                step(i, i % unroll)

        def on(i, lag, count):
            return not isinstance(i, int) or 0 <= i - lag < count

        LAST = 4
        FIRST = 6

        block = ctx.enter_context(nc.Block())

        @block.sync
        def _(sp):
            def load_graph(g, b):
                freed(sp, "mask_ready", g)
                sp.dma_start(adj_sb[:, b, :, :], adj_tiles[bass.ds(g, 1)].rearrange("o p t j -> (o p) t j")
                             ).then_inc(graph_in[b], 16)
                sp.dma_start(X[:, bass.ds(g * T, T), :], x_tiles[:, bass.ds(g * T, T), :]).then_inc(graph_in[b], 16)

            load_graph(0, 0)
            sp.dma_start(Wsb[:], W).then_inc(s["weights_in"], 16)
            sp.dma_start(a_sb[:], a.rearrange("(k o) x -> o (k x)", k=2), allow_slow_non_contiguous=True).then_inc(s["weights_in"], 16)
            sp.dma_start(Wg_sb[:], Wg).then_inc(s["weights_in"], 16)
            sp.dma_start(bg_rep[:], bg.rearrange("(o e) -> o e", o=1).to_broadcast([P, E])).then_inc(s["weights_in"], 16)
            load_graph(1, 1)
            sp.dma_start(W1s.rearrange("p (e h) -> p e h", e=E), W1.rearrange("e d h -> d e h")).then_inc(s["ffn_weights_in"], 16)
            sp.dma_start(W2s, W2.rearrange("e (c p) d -> p (e c) d", p=P)).then_inc(s["ffn_weights_in"], 16)
            sp.dma_start(b1_rep[:].rearrange("p e h -> p (e h)"),
                         b1.rearrange("(o e) h -> o (e h)", o=1).to_broadcast([P, E * H])).then_inc(s["ffn_weights_in"], 16)
            sp.dma_start(b2_rep[:].rearrange("p e h -> p (e h)"),
                         b2.rearrange("(o e) h -> o (e h)", o=1).to_broadcast([P, E * D])).then_inc(s["ffn_weights_in"], 16)
            with sp.Fori(2, G - 1, 2) as g0:
                load_graph(g0, 0)
                load_graph(g0 + 1, 1)

            sp.wait_ge(s["consts_made"], 1)
            for t in range(E):
                sp.dma_start(xs[E * STRIDE + t * P:E * STRIDE + (t + 1) * P, :], pad_rows[:]).then_inc(s["pads_done"], 16)
            sp.wait_ge(s["tab_ready"], 1)
            for e in range(E):
                r = sp.value_load(base_i[0:1, e:e + 1], min_val=0, max_val=E * STRIDE - P)
                sp.dma_start(xs[bass.ds(r, P), :], pad_rows[:]).then_inc(s["pads_done"], 16)
            sp.wait_ge(s["pads_done"], 16 * 2 * E)
            for b in range(2):
                sp.wait_ge(rows_sent[b], 16 * T * K * G // 2)

            def load_tile(i, b):
                r = sp.value_load(row_i[0:1, bass.ds(i, 1)], min_val=0, max_val=XS_ROWS - P)
                if not isinstance(i, int) or i >= RING:
                    sp.wait_ge(tile_out[b], (i - b) * 2)
                sp.dma_start(xt[:, b, :], xs[bass.ds(r, P), :]).then_inc(tile_in[b], 16)

            steps_of(sp, RING, SLOTS, RING, 0, load_tile)

            for b in range(RING):
                sp.wait_ge(tile_out[b], 16 * SLOTS // RING)
            ybuf = Wstage[:].rearrange("p k (c n) -> p (k c) n", c=4)
            for c in range(NCH):
                if c >= 4:
                    sp.wait_ge(s["second_add"], c - 3)
                for k in range(K):
                    sp.dma_start(ybuf[:, (c % 4) * 2 + k, :].rearrange("p (n d) -> p n d", d=D),
                                 y_tiles[k][:, c * CH:(c + 1) * CH, :]).then_inc(y_in[c % 4], 16)
                if c >= 2:
                    sp.wait_ge(s["second_add"], c - 1)
                    sp.dma_start(out_tiles[:, (c - 2) * CH:(c - 1) * CH, :],
                                 X[:, (c - 2) * CH:(c - 1) * CH, :]).then_inc(s["stored"], 16)
            for c in range(NCH - 2, NCH):
                sp.wait_ge(s["second_add"], c + 1)
                sp.dma_start(out_tiles[:, c * CH:(c + 1) * CH, :],
                             X[:, c * CH:(c + 1) * CH, :]).then_inc(s["stored"], 16)
            sp.wait_ge(s["stored"], 16 * NCH)

        @block.gpsimd
        def _(pool):
            pool.memset(ident[:], 0.0)
            pool.memset(tri[:], 0.0)
            pool.memset(ones[:], 1.0)
            pool.memset(eps_t[:], EPS)
            pool.memset(pad_rows[:, 0:D + 1], 0.0)
            pool.memset(pad_rows[:, D + 1:D + 2].bitcast(I32), SKIP)
            pool.memset(low8[:], 0.0)
            pool.memset(rows[:], 0.0).then_inc(s["ident_zero"], 1)
            pool.wait_ge(s["ident_zero"], 1)
            pool.affine_select(out=ident[:], in_=ident[:], compare_op=ALU.not_equal, fill=1.0, base=0,
                               pattern=[[-1, P]], channel_multiplier=1)
            pool.affine_select(out=tri[:], in_=tri[:], compare_op=ALU.is_ge, fill=1.0, base=0,
                               pattern=[[-1, P]], channel_multiplier=1)
            pool.affine_select(out=low8[:], in_=low8[:], compare_op=ALU.is_gt, fill=1.0, base=0,
                               pattern=[[-1, E], [1, E]], channel_multiplier=0)
            pool.iota(iota_e[:], pattern=[[1, E]], base=0, channel_multiplier=0,
                      allow_small_or_imprecise_dtypes=True)
            pool.iota(base0[:], pattern=[[STRIDE, E]], base=0, channel_multiplier=0,
                      allow_small_or_imprecise_dtypes=True)
            pool.iota(edge[:], pattern=[[P, TILES]], base=0, channel_multiplier=0,
                      allow_small_or_imprecise_dtypes=True)
            pool.iota(tile_no[:], pattern=[[1, SLOTS]], base=0, channel_multiplier=0,
                      allow_small_or_imprecise_dtypes=True)
            pool.iota(row0[:], pattern=[[P, SLOTS]], base=0, channel_multiplier=0,
                      allow_small_or_imprecise_dtypes=True)
            pool.iota(dest[:], pattern=[[P, T], [TOK, K]], base=0, channel_multiplier=1,
                      allow_small_or_imprecise_dtypes=True).then_inc(s["consts_made"], 1)

            def send_rows(g, b):
                ready(pool, "slots_ready", g)
                alone(pool)
                for t in range(T):
                    for k in range(K):
                        pool.indirect_dma_start(xs, bass.IndirectOffsetOnAxis(ap=slot[:, b, t, k:k + 1], axis=0),
                                                rows[:, b, t, k, :], None).then_inc(rows_sent[b], 16)

            steps_of(pool, 2, G, 2, 0, send_rows)

            def send_tile(i, b):
                ready(pool, "y_scaled", i)
                alone(pool)
                pool.indirect_dma_start(ytok, bass.IndirectOffsetOnAxis(ap=xt[:, b, D + 1:D + 2].bitcast(I32), axis=0),
                                        ys[:, b, :], None, bounds_check=SKIP - 1, oob_is_err=False
                                        ).then_inc(tile_out[b], 16)

            steps_of(pool, RING, SLOTS, RING, 0, send_tile)

        @block.tensor
        def _(pe):
            pe.wait_ge(s["consts_made"], 1)
            pe.wait_ge(s["weights_in"], 64)
            nc.tensor.transpose(bank[0][:, 0:P], Wsb[:], ident[:]).then_inc(s["wt_ps"], 1)
            pe.wait_ge(s["wt_sb"], 1)
            nc.tensor.matmul(bank[1][:, 0:2], WT[:], a_sb[:], start=True, stop=True).then_inc(s["wa_ps"], 1)
            pe.wait_ge(s["wrep_ready"], 2)

            def transpose_xhat(g, b):
                ready(pe, "xhat_ready", g)
                freed(pe, "xhat_t_sb", g, 1)
                for t in range(T):
                    m = nc.tensor.transpose(bank[0][:, t * P:(t + 1) * P], xhat[:, b, t, :], ident[:])
                m.then_inc(s["xhat_t_ps"], 1)

            def project(g, b):
                ready(pe, "xhat_t_sb", g)
                freed(pe, "h_sb", g, 1)
                for t in range(T):
                    m = nc.tensor.matmul(bank[1][:, t * (D + 2):(t + 1) * (D + 2)], xhatT[:, b, t * P:(t + 1) * P],
                                         Waug[:], start=True, stop=True)
                m.then_inc(s["h_ps"], 1)
                freed(pe, "relu_sb", g, 1)
                nc.tensor.matmul(bank[2][:, 0:N], wa2[:], xhatT[:, b, :], start=True, stop=True).then_inc(s["dst_ps"], 1)

            def transpose_p(g, b):
                ready(pe, "p_ready", g)
                freed(pe, "p_t_sb", g, 1)
                for j in range(T):
                    for t in range(T):
                        m = nc.tensor.transpose(bank[3][:, j * N + t * P:j * N + (t + 1) * P],
                                                p_sb[:, b, t, j * P:(j + 1) * P], ident[:])
                m.then_inc(s["p_t_ps"], 1)

            def attend(g, b):
                ready(pe, "p_t_sb", g)
                freed(pe, "x1_ready", g, 1)
                for t in range(T):
                    for j in range(T):
                        m = nc.tensor.matmul(bank[4][:, t * D:(t + 1) * D], pT[:, b, j, t * P:(t + 1) * P],
                                             h_sb[:, b, j, 0:D], start=(j == 0), stop=(j == T - 1))
                m.then_inc(s["attn_ps"], 1)

            def transpose_xn(g, b):
                ready(pe, "rows_ready", g)
                freed(pe, "xn_t_sb", g, 1)
                for t in range(T):
                    m = nc.tensor.transpose(bank[5][:, t * P:(t + 1) * P], rows[:, b, t, 0, 0:D], ident[:])
                m.then_inc(s["xn_t_ps"], 1)

            def gate(g, b):
                ready(pe, "xn_t_sb", g)
                freed(pe, "logits_sb", g, 1)
                for t in range(T):
                    m = nc.tensor.matmul(bank[6][:, t * E:(t + 1) * E], xnT[:, b, t * P:(t + 1) * P], Wg_sb[:],
                                         start=True, stop=True)
                m.then_inc(s["logits_ps"], 1)

            def count(g, b):
                ready(pe, "sel_ready", g)
                freed(pe, "base_ready", g, 1)
                c = bank[7]
                nc.tensor.matmul(c[:, 0:E], tri[:], sel[:, b, 0, :], start=True, stop=True)
                nc.tensor.matmul(c[:, E:2 * E], tri[:], sel[:, b, 1, :], start=True, stop=False)
                nc.tensor.matmul(c[:, E:2 * E], ones[:], sel[:, b, 0, :], start=False, stop=True)
                nc.tensor.matmul(c[:, 2 * E:3 * E], ones[:], sel[:, b, 0, :], start=True, stop=False)
                nc.tensor.matmul(c[:, 2 * E:3 * E], ones[:], sel[:, b, 1, :], start=False, stop=True
                                 ).then_inc(s["count_ps"], 1)

            def first_layer(i, j):
                b = j % 2
                if on(i, 0, G):
                    transpose_xhat(i, b)
                if on(i, 4, G):
                    count(i - 4, b)
                if on(i, 2, G):
                    transpose_p(i - 2, b)
                if on(i, 3, G):
                    transpose_xn(i - 3, 1 - b)
                if on(i, 0, G):
                    project(i, b)
                if on(i, 3, G):
                    gate(i - 3, 1 - b)
                if on(i, 2, G):
                    attend(i - 2, b)

            steps_of(pe, FIRST, G, 2, LAST, first_layer)

            pe.wait_ge(s["tab_ready"], 1)
            pe.wait_ge(s["base_ready"], G)
            pe.wait_ge(s["w1_lo"], G)
            pe.wait_ge(s["w2_lo"], G)

            def turn_x(i, b, r):
                pe.wait_ge(tile_in[r], (i - r) * 2 + 16)
                freed(pe, "xt_lo", i)
                nc.tensor.transpose(bank[b][:, 0:P], xt[:, r, 0:D], ident[:]).then_inc(s["xt_ps"], 1)

            def up(i, b):
                e = pe.value_load(eid_i[0:1, bass.ds(i, 1)], min_val=0, max_val=E - 1)
                ready(pe, "xt_lo", i)
                freed(pe, "biased", i)
                hi, lo = W1hi[:, bass.ds(e * H, H)], W1lo[:, bass.ds(e * H, H)]
                o = bank[2 + b]
                nc.tensor.matmul(o[:], xTh[:, b, :], hi, start=True, stop=False)
                nc.tensor.matmul(o[:], xTh[:, b, :], lo, start=False, stop=False)
                nc.tensor.matmul(o[:], xTl[:, b, :], hi, start=False, stop=True).then_inc(s["up_ps"], 1)

            def turn_g(i, b):
                ready(pe, "gelu_done", i)
                freed(pe, "gt_lo", i)
                for c in range(C):
                    m = nc.tensor.transpose(bank[4 + b][:, c * P:(c + 1) * P], g_sb[:, b, c * P:(c + 1) * P], ident[:])
                m.then_inc(s["gt_ps"], 1)

            def down(i, b):
                e = pe.value_load(eid_i[0:1, bass.ds(i, 1)], min_val=0, max_val=E - 1)
                ready(pe, "gt_lo", i)
                freed(pe, "y_full", i)
                o = bank[6 + b]
                W2f = W2hl[:].rearrange("p b k d -> p (b k d)")
                for c in range(C):
                    nc.tensor.matmul(o[:, 0:2 * D], gTh[:, b, c * P:(c + 1) * P],
                                     W2f[:, bass.ds(e * (C * 2 * D) + c * 2 * D, 2 * D)],
                                     start=(c == 0), stop=False)
                    m = nc.tensor.matmul(o[:, 0:D], gTl[:, b, c * P:(c + 1) * P],
                                         W2f[:, bass.ds(e * (C * 2 * D) + c * 2 * D, D)],
                                         start=False, stop=(c == C - 1))
                m.then_inc(s["down_ps"], 1)

            def expert_step(i, j):
                b = j % 2
                if on(i, 0, SLOTS):
                    turn_x(i, b, j)
                if on(i, 1, SLOTS):
                    up(i - 1, 1 - b)
                if on(i, 2, SLOTS):
                    turn_g(i - 2, b)
                if on(i, 3, SLOTS):
                    down(i - 3, 1 - b)

            steps_of(pe, RING, SLOTS, RING, 3, expert_step)

        @block.scalar
        def _(act):
            act.wait_ge(s["wt_ps"], 1)
            nc.scalar.activation(WT[:], bank[0][:, 0:P], ACT.Copy).then_inc(s["wt_sb"], 1)

            def root(g, b, mv, rt, stats, log, done):
                ready(act, stats, g)
                nc.scalar.activation(rt[:, b, 0, :], mv[:, b, :, 1], ACT.Ln, bias=eps_t[:, 0:1]).then_inc(s[log], 1)
                ready(act, log, g)
                nc.scalar.activation(rt[:, b, 1, :], rt[:, b, 0, :], ACT.Exp, scale=-0.5).then_inc(s[done], 1)

            def take_scores(g, b):
                ready(act, "h_ps", g)
                freed(act, "attn_ps", g)
                nc.scalar.activation(h_sb[:, b, :, :].rearrange("p t d -> p (t d)"), bank[1][:, 0:T * (D + 2)],
                                     ACT.Copy).then_inc(s["h_sb"], 1)
                ready(act, "dst_ps", g)
                freed(act, "e_sum", g)
                nc.scalar.activation(dst_sb[:, b, :], bank[2][:, 0:N], ACT.Copy, scale=SLOPE).then_inc(s["dst_sb"], 1)
                ready(act, "h_sb", g)
                for t in range(T):
                    m = nc.scalar.activation(relu_sb[:, b, t, :], bank[2][:, 0:N], ACT.Relu,
                                             bias=h_sb[:, b, t, D:D + 1], scale=1.0 - SLOPE)
                m.then_inc(s["relu_sb"], 1)

            def exps(g, b):
                ready(act, "negmax_ready", g)
                freed(act, "p_t_ps", g)
                freed(act, "rinv_ready", g)
                for t in range(T):
                    m = nc.scalar.activation(p_sb[:, b, t, :], e_sb[:, b, t, :], ACT.Exp, bias=nmax[:, b, t:t + 1],
                                             accum_out=psums[:, b, t:t + 1])
                m.then_inc(s["p_ready"], 1)

            def copy_out(g, b, ps, dst, src, done, user):
                ready(act, ps, g)
                freed(act, user, g)
                nc.scalar.activation(dst, src, ACT.Copy).then_inc(s[done], 1)

            def gate_exp(g, b):
                ready(act, "gap_ready", g)
                nc.scalar.activation(gap[:, b, 1, :], gap[:, b, 0, :], ACT.Exp).then_inc(s["gap_exp"], 1)

            def split_weights(g):
                if isinstance(g, int) and g == 0:
                    act.wait_ge(s["ffn_weights_in"], 64)
                nc.scalar.activation(W1hi[:, bass.ds(g * P, P)], W1s[:, bass.ds(g * P, P)], ACT.Copy
                                     ).then_inc(s["w1_hi"], 1)
                nc.scalar.activation(W2hl[:, bass.ds(g, 1), 0, :].rearrange("p o d -> p (o d)"),
                                     W2s[:, bass.ds(g, 1), :].rearrange("p o d -> p (o d)"), ACT.Copy
                                     ).then_inc(s["w2_hi"], 1)

            def first_layer(i, j):
                b = j % 2
                if on(i, 3, G):
                    root(i - 3, 1 - b, mv2, rt2, "ln2_mv", "ln2_log", "ln2_root")
                if on(i, 0, G):
                    root(i, b, mv1, rt1, "ln1_mv", "ln1_log", "ln1_root")
                if on(i, 2, G):
                    exps(i - 2, b)
                if on(i, 1, G):
                    take_scores(i - 1, 1 - b)
                if on(i, 0, G):
                    copy_out(i, b, "xhat_t_ps", xhatT[:, b, :], bank[0][:, 0:N], "xhat_t_sb", "dst_ps")
                if on(i, 4, G):
                    gate_exp(i - 4, b)
                if on(i, 2, G):
                    copy_out(i - 2, b, "p_t_ps", pT[:, b, :, :].rearrange("p j n -> p (j n)"), bank[3][:],
                             "p_t_sb", "attn_ps")
                if on(i, 3, G):
                    copy_out(i - 3, 1 - b, "xn_t_ps", xnT[:, 1 - b, :], bank[5][:, 0:N], "xn_t_sb", "logits_ps")
                if on(i, 4, G):
                    split_weights(i - 4)

            steps_of(act, FIRST, G, 2, LAST, first_layer)

            def expert_step(i, j):
                b = j % 2
                if on(i, 4, SLOTS):
                    n, r = i - 4, (j - 4) % RING
                    ready(act, "y_full", n)
                    if isinstance(i, int):
                        if n >= RING:
                            act.wait_ge(tile_out[r], n // RING * 16)
                    elif j >= 4:
                        act.wait_ge(tile_out[r], (i - j) * 2)
                    else:
                        before_loop_round(i, j, r)
                    nc.scalar.activation(ys[:, r, :], yb[:, b, :], ACT.Copy, scale=xt[:, r, D:D + 1]
                                         ).then_inc(s["y_scaled"], 1)
                if on(i, 0, SLOTS):
                    ready(act, "xt_ps", i)
                    freed(act, "up_ps", i)
                    nc.scalar.activation(xTh[:, b, :], bank[b][:, 0:P], ACT.Copy).then_inc(s["xt_hi"], 1)
                if on(i, 1, SLOTS):
                    ready(act, "biased", i - 1)
                    freed(act, "gt_ps", i - 1)
                    nc.scalar.activation(g_sb[:, 1 - b, :], hb[:, 1 - b, :], ACT.Gelu).then_inc(s["gelu_done"], 1)
                if on(i, 2, SLOTS):
                    ready(act, "gt_ps", i - 2)
                    freed(act, "down_ps", i - 2)
                    nc.scalar.activation(gTh[:, b, :], bank[4 + b][:], ACT.Copy).then_inc(s["gt_hi"], 1)

            def before_loop_round(i, j, r):
                act.wait_ge(tile_out[r], (i - j) * 2 - 16)

            steps_of(act, 2 * RING, SLOTS, RING, 4, expert_step)

        @block.vector
        def _(dve):
            dve.wait_ge(s["consts_made"], 1)
            dve.tensor_copy(base[:], base0[:]).then_inc(s["base_init"], 1)
            dve.wait_ge(s["wa_ps"], 1)
            dve.tensor_scalar(Waug[:, D:D + 2], bank[1][:, 0:2], 1.0 - SLOPE, None, ALU.mult).then_inc(s["wrep_ready"], 1)
            dve.tensor_copy(Waug[:, 0:D], Wsb[:]).then_inc(s["wa_sb"], 1)
            dve.tensor_copy(wa2[:], bank[1][:, 1:2].to_broadcast([P, P])).then_inc(s["wrep_ready"], 1)
            dve.wait_ge(s["wa_sb"], 1)
            dve.wait_ge(s["base_init"], 1)

            def stats(g, b, src, st, mv, n_stats, n_mv):
                for t in range(T):
                    m = dve.bn_stats(st[:, b, t, :], src(t))
                m.then_inc(s[n_stats], 1)
                ready(dve, n_stats, g)
                alone(dve)
                for t in range(T):
                    m = dve.bn_aggr(mv[:, b, t, :], st[:, b, t, :])
                m.then_inc(s[n_mv], 1)

            def newton(g, b, mv, rt, name):
                ready(dve, f"{name}_root", g)
                ready(dve, f"{name}_mv", g)
                dve.scalar_tensor_tensor(out=rt[:, b, 2, :], in0=mv[:, b, :, 1], scalar=EPS, in1=rt[:, b, 1, :],
                                         op0=ALU.add, op1=ALU.mult).then_inc(s[f"{name}_n1"], 1)
                ready(dve, f"{name}_n1", g)
                dve.scalar_tensor_tensor(out=rt[:, b, 3, :], in0=rt[:, b, 2, :], scalar=-0.5, in1=rt[:, b, 1, :],
                                         op0=ALU.mult, op1=ALU.mult).then_inc(s[f"{name}_n2"], 1)
                ready(dve, f"{name}_n2", g)
                dve.scalar_tensor_tensor(out=rt[:, b, 2, :], in0=rt[:, b, 3, :], scalar=1.5, in1=rt[:, b, 1, :],
                                         op0=ALU.add, op1=ALU.mult).then_inc(s[f"{name}_rstd"], 1)
                ready(dve, f"{name}_rstd", g)

            def norm1(g, b):
                newton(g, b, mv1, rt1, "ln1")
                freed(dve, "xhat_t_ps", g)
                for t in range(T):
                    m = dve.tensor_scalar(xhat[:, b, t, :], X[:, bass.ds(g * T + t, 1), :].rearrange("p o d -> p (o d)"),
                                          mv1[:, b, t, 0:1], rt1[:, b, 2, t:t + 1], ALU.subtract, ALU.mult)
                m.then_inc(s["xhat_ready"], 1)

            def norm2(g, b, r):
                newton(g, b, mv2, rt2, "ln2")
                if not isinstance(g, int) or g >= 2:
                    dve.wait_ge(rows_sent[b], (g - r) * 32)
                for t in range(T):
                    m = dve.tensor_scalar(rows[:, b, t, :, 0:D],
                                          X[:, bass.ds(g * T + t, 1), :].to_broadcast([P, K, D]),
                                          mv2[:, b, t, 0:1], rt2[:, b, 2, t:t + 1], ALU.subtract, ALU.mult)
                m.then_inc(s["rows_ready"], 1)

            def scores(g, b):
                freed(dve, "e_max", g)
                dve.tensor_scalar(mask[:, b, :, :], adj_sb[:, b, :, :], 0.0, NEG, ALU.is_le, ALU.mult
                                  ).then_inc(s["mask_ready"], 1)
                ready(dve, "relu_sb", g)
                freed(dve, "p_ready", g)
                for t in range(T):
                    m = dve.tensor_tensor(e_sb[:, b, t, :], relu_sb[:, b, t, :], dst_sb[:, b, :], ALU.add)
                m.then_inc(s["e_sum"], 1)
                ready(dve, "e_sum", g)
                ready(dve, "mask_ready", g)
                alone(dve)
                for t in range(T):
                    m = dve.tensor_tensor_reduce(e_sb[:, b, t, :], e_sb[:, b, t, :], mask[:, b, t, :], 1.0, -3.0e38,
                                                 ALU.add, ALU.max, emax[:, b, t:t + 1])
                m.then_inc(s["e_max"], 1)
                ready(dve, "e_max", g)
                dve.tensor_scalar(nmax[:, b, :], emax[:, b, :], -1.0, None, ALU.mult).then_inc(s["negmax_ready"], 1)

            def residual(g, b):
                ready(dve, "p_ready", g)
                dve.reciprocal(rinv[:, b, :], psums[:, b, :]).then_inc(s["rinv_ready"], 1)
                ready(dve, "rinv_ready", g)
                ready(dve, "attn_ps", g)
                for t in range(T):
                    xg = X[:, bass.ds(g * T + t, 1), :].rearrange("p o d -> p (o d)")
                    m = dve.scalar_tensor_tensor(out=xg, in0=bank[4][:, t * D:(t + 1) * D], scalar=rinv[:, b, t:t + 1],
                                                 in1=xg, op0=ALU.mult, op1=ALU.add)
                m.then_inc(s["x1_ready"], 1)
                ready(dve, "x1_ready", g)
                alone(dve)
                stats(g, b, lambda t: X[:, bass.ds(g * T + t, 1), :].rearrange("p o d -> p (o d)"),
                      st2, mv2, "ln2_stats", "ln2_mv")

            def top_two(g, b):
                ready(dve, "logits_ps", g)
                for t in range(T):
                    m = dve.tensor_tensor(lg[:, b, t, :], bank[6][:, t * E:(t + 1) * E], bg_rep[:], ALU.add)
                m.then_inc(s["logits_sb"], 1)
                ready(dve, "logits_sb", g)
                alone(dve)
                for t in range(T):
                    m = dve.max(top[:, b, t, :], lg[:, b, t, :])
                m.then_inc(s["top_ready"], 1)
                ready(dve, "top_ready", g)
                alone(dve)
                for t in range(T):
                    m = dve.max_index(topi[:, b, t, :], top[:, b, t, :], lg[:, b, t, :])
                m.then_inc(s["index_ready"], 1)
                dve.tensor_tensor(gap[:, b, 0, :], top[:, b, :, 1], top[:, b, :, 0], ALU.subtract
                                  ).then_inc(s["gap_ready"], 1)
                ready(dve, "index_ready", g)
                dve.tensor_copy(pick[:, b, :, :], topi[:, b, :, 0:K]).then_inc(s["picks_ready"], 1)

            def select(g, b):
                ready(dve, "picks_ready", g)
                for t in range(T):
                    for k in range(K):
                        m = dve.tensor_scalar(hot[:, b, t, k, :], iota_e[:], pick[:, b, t, k:k + 1], None, ALU.is_equal)
                m.then_inc(s["onehot_ready"], 1)
                ready(dve, "onehot_ready", g)
                freed(dve, "count_ps", g)
                dve.tensor_tensor(sel[:, b, :, :], hot[:, b, :, 0, :], hot[:, b, :, 1, :], ALU.add
                                  ).then_inc(s["sel_ready"], 1)

            def place(g, b):
                ready(dve, "gap_exp", g)
                dve.tensor_scalar(gap[:, b, 2, :], gap[:, b, 1, :], 1.0, None, ALU.add).then_inc(s["gate_den"], 1)
                ready(dve, "gate_den", g)
                dve.reciprocal(rows[:, b, :, 0, D], gap[:, b, 2, :]).then_inc(s["gate_first"], 1)
                ready(dve, "gate_first", g)
                dve.tensor_tensor(rows[:, b, :, 1, D], rows[:, b, :, 0, D], gap[:, b, 1, :], ALU.mult
                                  ).then_inc(s["gates_ready"], 1)
                dve.tensor_copy(rows[:, b, :, :, D + 1].bitcast(I32), dest[:]).then_inc(s["dest_ready"], 1)
                ready(dve, "dest_ready", g)
                dve.tensor_scalar(dest[:], dest[:], float(N), None, ALU.add).then_inc(s["dest_moved"], 1)
                ready(dve, "count_ps", g)
                if not isinstance(g, int) or g >= 1:
                    dve.wait_ge(s["base_ready"], g)
                for t in range(T):
                    m = dve.tensor_tensor(pos[:, b, t, :], bank[7][:, t * E:(t + 1) * E], base[:], ALU.add)
                m.then_inc(s["pos_ready"], 1)
                ready(dve, "pos_ready", g)
                dve.tensor_tensor(base[:], bank[7][:, 2 * E:3 * E], base[:], ALU.add).then_inc(s["base_ready"], 1)
                for k in range(K):
                    m = dve.tensor_tensor(posm[:, b, :, k, :], hot[:, b, :, k, :], pos[:, b, :, :], ALU.mult)
                m.then_inc(s["posmask_ready"], 1)
                ready(dve, "posmask_ready", g)
                ready(dve, "gates_ready", g)
                ready(dve, "dest_moved", g)
                with nc.allow_low_precision(reason="a sum of one row number and zeros, all whole"):
                    dve.tensor_reduce(slot[:, b, :, :], posm[:, b, :, :, :], AX.X, ALU.add).then_inc(s["slots_ready"], 1)

            def split_weights(g):
                ready(dve, "w1_hi", g)
                dve.tensor_tensor(W1lo[:, bass.ds(g * P, P)], W1s[:, bass.ds(g * P, P)],
                                  W1hi[:, bass.ds(g * P, P)].bitcast(F32), ALU.subtract).then_inc(s["w1_lo"], 1)
                ready(dve, "w2_hi", g)
                dve.tensor_tensor(W2hl[:, bass.ds(g, 1), 1, :].rearrange("p o d -> p (o d)"),
                                  W2s[:, bass.ds(g, 1), :].rearrange("p o d -> p (o d)"),
                                  W2hl[:, bass.ds(g, 1), 0, :].rearrange("p o d -> p (o d)").bitcast(F32),
                                  ALU.subtract).then_inc(s["w2_lo"], 1)

            def first_layer(i, j):
                b = j % 2
                if on(i, 0, G):
                    dve.wait_ge(graph_in[b], (i - b) * 16 + 32)
                    alone(dve)
                    stats(i, b, lambda t: X[:, bass.ds(i * T + t, 1), :].rearrange("p o d -> p (o d)"),
                          st1, mv1, "ln1_stats", "ln1_mv")
                if on(i, 4, G):
                    top_two(i - 4, b)
                if on(i, 0, G):
                    norm1(i, b)
                if on(i, 4, G):
                    select(i - 4, b)
                if on(i, 3, G):
                    norm2(i - 3, 1 - b, 1 - b)
                if on(i, 1, G):
                    scores(i - 1, 1 - b)
                if on(i, 4, G):
                    place(i - 4, b)
                if on(i, 2, G):
                    residual(i - 2, b)
                if on(i, 4, G):
                    split_weights(i - 4)

            steps_of(dve, FIRST, G, 2, LAST, first_layer)

            dve.wait_ge(s["base_ready"], G)
            dve.tensor_tensor(cnt[:], base[0:1, :], base0[0:1, :], ALU.subtract).then_inc(s["cnt_ready"], 1)
            dve.tensor_copy(base_i[:], base[0:1, :]).then_inc(s["tab_f"], 1)
            dve.wait_ge(s["cnt_ready"], 1)
            dve.tensor_tensor(over[:], cnt[:].rearrange("o (e x) -> o e x", x=1).to_broadcast([1, E, TILES]),
                              edge[:].rearrange("o (x n) -> o x n", x=1).to_broadcast([1, E, TILES]),
                              ALU.is_gt).then_inc(s["over_ready"], 1)
            dve.wait_ge(s["over_ready"], 1)
            dve.tensor_reduce(ntile[:], over[:], AX.X, ALU.add).then_inc(s["ntile_ready"], 1)
            dve.wait_ge(s["ntile_ready"], 1)
            dve.tensor_tensor(ntri[:], low8[:], ntile[:].rearrange("o (x e) -> o x e", x=1).to_broadcast([1, E, E]),
                              ALU.mult).then_inc(s["ntri_ready"], 1)
            dve.tensor_scalar(span[:], ntile[:], -float(P), float(STRIDE), ALU.mult, ALU.add
                              ).then_inc(s["span_ready"], 1)
            dve.wait_ge(s["ntri_ready"], 1)
            dve.tensor_reduce(cumend[:], ntri[:], AX.X, ALU.add).then_inc(s["cumend_ready"], 1)
            dve.wait_ge(s["cumend_ready"], 1)
            dve.tensor_tensor(comp[:], tile_no[:].rearrange("o (n x) -> o n x", x=1).to_broadcast([1, SLOTS, E]),
                              cumend[:].rearrange("o (x e) -> o x e", x=1).to_broadcast([1, SLOTS, E]),
                              ALU.is_ge).then_inc(s["comp_ready"], 1)
            dve.wait_ge(s["comp_ready"], 1)
            dve.wait_ge(s["span_ready"], 1)
            dve.tensor_reduce(eid[:], comp[:], AX.X, ALU.add).then_inc(s["eid_ready"], 1)
            dve.tensor_tensor(compm[:], comp[:], span[:].rearrange("o (x e) -> o x e", x=1).to_broadcast([1, SLOTS, E]),
                              ALU.mult).then_inc(s["spanmul_ready"], 1)
            dve.wait_ge(s["spanmul_ready"], 1)
            dve.tensor_reduce(rowsum[:], compm[:], AX.X, ALU.add).then_inc(s["rowsum_ready"], 1)
            dve.wait_ge(s["eid_ready"], 1)
            dve.tensor_scalar(eid_i[:, 0:SLOTS], eid[:], float(E - 1), None, ALU.min).then_inc(s["tab_f"], 1)
            dve.wait_ge(s["rowsum_ready"], 1)
            dve.tensor_tensor(row_i[:, 0:SLOTS], rowsum[:], row0[:], ALU.add).then_inc(s["tab_f"], 1)
            dve.wait_ge(s["tab_f"], 3)
            dve.nop().then_inc(s["tab_ready"], 1)

            def expert_step(i, j):
                b = j % 2
                if on(i, 0, SLOTS):
                    ready(dve, "xt_hi", i)
                    dve.tensor_tensor(xTl[:, b, :], bank[b][:, 0:P], xTh[:, b, :].bitcast(F32), ALU.subtract
                                      ).then_inc(s["xt_lo"], 1)
                if on(i, 1, SLOTS):
                    n, q = i - 1, 1 - b
                    e = dve.value_load(eid_i[0:1, bass.ds(n, 1)], min_val=0, max_val=E - 1)
                    ready(dve, "up_ps", n)
                    freed(dve, "gelu_done", n)
                    dve.tensor_tensor(hb[:, q, :], bank[2 + q][:],
                                      b1_rep[:, bass.ds(e, 1), :].rearrange("p o h -> p (o h)"), ALU.add
                                      ).then_inc(s["biased"], 1)
                if on(i, 2, SLOTS):
                    ready(dve, "gt_hi", i - 2)
                    dve.tensor_tensor(gTl[:, b, :], bank[4 + b][:], gTh[:, b, :].bitcast(F32), ALU.subtract
                                      ).then_inc(s["gt_lo"], 1)
                if on(i, 3, SLOTS):
                    n, q = i - 3, 1 - b
                    e = dve.value_load(eid_i[0:1, bass.ds(n, 1)], min_val=0, max_val=E - 1)
                    ready(dve, "down_ps", n)
                    dve.tensor_tensor(ya[:, q, :], bank[6 + q][:, 0:D],
                                      b2_rep[:, bass.ds(e, 1), :].rearrange("p o h -> p (o h)"), ALU.add
                                      ).then_inc(s["y_half"], 1)
                    ready(dve, "y_half", n)
                    freed(dve, "y_scaled", n)
                    dve.tensor_tensor(yb[:, q, :], bank[6 + q][:, D:2 * D], ya[:, q, :], ALU.add
                                      ).then_inc(s["y_full"], 1)

            steps_of(dve, RING, SLOTS, RING, 3, expert_step)

            ybuf = Wstage[:].rearrange("p k (c n) -> p (k c) n", c=4)
            for c in range(NCH):
                xc = X[:, c * CH:(c + 1) * CH, :].rearrange("p n d -> p (n d)")
                dve.wait_ge(y_in[c % 4], 32 * (c // 4 + 1))
                dve.tensor_tensor(xc, xc, ybuf[:, (c % 4) * 2, :], ALU.add).then_inc(s["first_add"], 1)
                dve.wait_ge(s["first_add"], c + 1)
                dve.tensor_tensor(xc, xc, ybuf[:, (c % 4) * 2 + 1, :], ALU.add).then_inc(s["second_add"], 1)


_INS = ['x', 'adj', 'L0_gnn_W', 'L0_gnn_a', 'L0_ffn_Wg', 'L0_ffn_bg', 'L0_ffn_W1', 'L0_ffn_b1', 'L0_ffn_W2', 'L0_ffn_b2']


def kernel(**inputs):
    import numpy as _np
    import concourse.bacc as _bacc
    from concourse import mybir as _mybir
    from concourse.bass_utils import run_bass_kernel_spmd as _run

    nc = _bacc.Bacc("TRN2", target_bir_lowering=False, num_devices=1)
    arrays, args = {}, []
    for name in _INS:
        v = _np.ascontiguousarray(inputs[name])
        arrays[f"in_{name}_dram"] = v
        args.append(nc.dram_tensor(f"in_{name}_dram", v.shape, _mybir.dt.from_np(v.dtype), kind="ExternalInput").ap())
    args.append(nc.dram_tensor("out_dram", (G, N, D), _mybir.dt.float32, kind="ExternalOutput").ap())
    build(nc, *args)
    r = _run(nc, [arrays], core_ids=[0])
    return r.results[0]["out_dram"]
```

```python
from contextlib import ExitStack

import concourse.bass as bass
from concourse import mybir

F32 = mybir.dt.float32
F32R = mybir.dt.float32r
BF16 = mybir.dt.bfloat16
I32 = mybir.dt.int32
U32 = mybir.dt.uint32
ALU = mybir.AluOpType
ACT = mybir.ActivationFunctionType
AX = mybir.AxisListType

P = 128
G, N, D = 32, 256, 128
T = N // P
E, H, K = 8, 512, 2
C = H // P
TOK = G * N
TILES = TOK // P
ROW = D + 2
STRIDE = TOK + P
SLOTS = TOK * K // P + E
PAD_ROWS = (E) * P
XS_ROWS = E * STRIDE + PAD_ROWS
SKIP = TOK * K
NEG = -9000000000000000.0
SLOPE = 0.2
EPS = 1e-5
RB = 4
RING = 8
CH = 8
NCH = TILES // CH

SEMAPHORES = """
    consts_made ident_zero weights_in ffn_weights_in wt_ps wt_sb wa_ps wa_sb wrep_ready
    ln1_stats ln2_stats moments_ready log_ready root_ready newton1 newton2 rstd_ready
    shift_ready xhat_ready xhat_t_ps xhat_t_sb h_ps dst_ps h_sb dst_sb relu_sb
    mask_ready e_sum e_max negmax_ready p_ready rinv_ready p_t_ps p_t_sb attn_ps
    x1_ready rows_ready
    xn_t_ps xn_t_sb logits_ps logits_sb top_ready index_ready picks_ready gap_ready gap_exp
    gate_den gate_first gates_ready onehot_ready sel_ready count_ps pos_ready posmask_ready
    slots_ready base_ready dest_ready dest_moved base_init dest_init
    w1_hi w2_hi w1_lo w2_lo
    cnt_ready over_ready ntile_ready ntri_ready cumend_ready comp_ready eid_ready span_ready
    spanmul_ready rowsum_ready tab_f tab_ready pads_done dummy_done
    xt_ps xt_hi xt_lo up_ps biased gelu_done gt_ps gt_hi gt_lo down_ps y_half y_full y_scaled
    first_add second_add stored passed_pool passed_dve
""".split()


def build(nc, x, adj, W, a, Wg, bg, W1, b1, W2, b2, out):
    xs = nc.dram_tensor("routed_rows", (XS_ROWS, ROW), F32, kind="Internal").ap()
    ytok = nc.dram_tensor("expert_out", (K * TOK, D), F32, kind="Internal").ap()
    x_tiles = x.rearrange("g (t p) d -> p (g t) d", p=P)
    out_tiles = out.rearrange("g (t p) d -> p (g t) d", p=P)
    adj_tiles = adj.rearrange("g (t p) j -> g p t j", p=P)
    y_tiles = ytok.rearrange("(k n p) d -> k p n d", k=K, p=P)

    with ExitStack() as ctx:
        def sb(name, shape, dt=F32):
            return ctx.enter_context(nc.sbuf_tensor(name, shape, dt))

        s = {n: ctx.enter_context(nc.semaphore(n)) for n in SEMAPHORES}
        x_in = [ctx.enter_context(nc.semaphore(f"x_in{i}")) for i in range(2)]
        adj_in = [ctx.enter_context(nc.semaphore(f"adj_in{i}")) for i in range(2)]
        rows_sent = [ctx.enter_context(nc.semaphore(f"rows_sent{i}")) for i in range(RB)]
        tile_in = [ctx.enter_context(nc.semaphore(f"tile_in{i}")) for i in range(RING)]
        tile_out = [ctx.enter_context(nc.semaphore(f"tile_out{i}")) for i in range(RING)]
        y_in = [ctx.enter_context(nc.semaphore(f"y_in{i}")) for i in range(4)]

        bank = [ctx.enter_context(nc.psum_tensor(f"bank{i}", [P, 512], F32)) for i in range(8)]

        X = sb("X", [P, TILES, D])
        ident = sb("ident", [P, P])
        tri = sb("tri", [P, P], BF16)
        ones = sb("ones", [P, P], BF16)
        iota_e = sb("iota_e", [P, E])
        Waug = sb("Waug", [P, D + 2])
        Wsb = sb("Wsb", [P, D])
        WT = sb("WT", [P, P])
        a_sb = sb("a_sb", [P, 2])
        wa2 = sb("wa2", [P, P])
        Wg_sb = sb("Wg_sb", [P, E])
        bg_rep = sb("bg_rep", [P, E])
        b1_rep = sb("b1_rep", [P, E, H])
        b2_rep = sb("b2_rep", [P, E, D])
        Wstage = sb("Wstage", [P, 2, E * H])
        W1hi = sb("W1hi", [P, E * H], F32R)
        W1lo = sb("W1lo", [P, E * H], F32R)
        W2hl = sb("W2hl", [P, E * C, 2, D], F32R)
        W1s = Wstage[:, 0, :]
        W2s = Wstage[:, 1, :].rearrange("p (b d) -> p b d", d=D)

        adj_sb = sb("adj_sb", [P, 2, T, N])
        stat = sb("stat", [P, 2, 2, T, 6])
        mean_var = sb("mean_var", [P, 2, 2, T, 2])
        root = sb("root", [P, 2, 4, 2, T])
        shift = sb("shift", [P, 2, T])
        xhat = sb("xhat", [P, 2, T, D])
        xhatT = sb("xhatT", [P, 2, N])
        h_sb = sb("h_sb", [P, 2, T, D + 2])
        dst_sb = sb("dst_sb", [P, 2, N])
        relu_sb = sb("relu_sb", [P, 2, T, N])
        e_sb = sb("e_sb", [P, 2, T, N])
        emax = sb("emax", [P, 2, T])
        nmax = sb("nmax", [P, 2, T])
        p_sb = sb("p_sb", [P, 2, T, N])
        psums = sb("psums", [P, 2, T])
        rinv = sb("rinv", [P, 2, T])
        pT = sb("pT", [P, 2, T, N])
        rows = sb("rows", [P, RB, T, K, ROW])
        xnT = sb("xnT", [P, 2, N])
        lg = sb("lg", [P, 2, T, E])
        top = sb("top", [P, 2, T, 8])
        topi = sb("topi", [P, 2, T, 8], U32)
        pick = sb("pick", [P, 2, T, K])
        gap = sb("gap", [P, 2, 4, T])
        hot = sb("hot", [P, 2, T, K, E])
        sel = sb("sel", [P, 2, T, E], BF16)
        pos = sb("pos", [P, 2, T, E])
        posm = sb("posm", [P, 2, T, K, E])
        slot = sb("slot", [P, RB, T, K], I32)
        base = sb("base", [P, E])
        base0 = sb("base0", [P, E])
        dest = sb("dest", [P, T, K])
        eps_t = sb("eps_t", [P, 1])

        cnt = sb("cnt", [1, E])
        edge = sb("edge", [1, TILES])
        ntile = sb("ntile", [1, E])
        low8 = sb("low8", [1, E, E])
        ntri = sb("ntri", [1, E, E])
        cumend = sb("cumend", [1, E])
        tile_no = sb("tile_no", [1, SLOTS])
        eid = sb("eid", [1, SLOTS])
        span = sb("span", [1, E])
        rowsum = sb("rowsum", [1, SLOTS])
        row0 = sb("row0", [1, SLOTS])
        eid_i = sb("eid_i", [1, SLOTS + 8], I32)
        row_i = sb("row_i", [1, SLOTS + 8], I32)
        base_i = sb("base_i", [1, E], I32)
        pad_rows = sb("pad_rows", [P, ROW])

        spare = Wstage[:].rearrange("p k n -> p (k n)")
        taken = [0]

        def part(*shape):
            n = 1
            for d in shape:
                n *= d
            taken[0] += n
            names = "abc"[:len(shape)]
            return spare[:, taken[0] - n:taken[0]].rearrange(
                f"p ({' '.join(names)}) -> p {' '.join(names)}", **dict(zip(names, shape)))

        xt = part(RING, ROW)
        xTh = sb("xTh", [P, 2, P], F32R)
        xTl = sb("xTl", [P, 2, P], F32R)
        hb = part(2, H)
        g_sb = part(2, H)
        gTh = sb("gTh", [P, 2, H], F32R)
        gTl = sb("gTl", [P, 2, H], F32R)
        ya = part(2, D)
        yb = part(2, D)
        ys = part(RING, D)
        comp = part(SLOTS, E)[0:1]
        compm = part(SLOTS, E)[0:1]
        over = part(E, TILES)[0:1]

        def ready(eng, name, g):
            eng.wait_ge(s[name], g + 1)

        def freed(eng, name, g, depth=2):
            if not isinstance(g, int) or g >= depth:
                eng.wait_ge(s[name], g + 1 - depth)

        def alone(eng):
            eng.sem_inc(s["passed_pool" if eng is nc.gpsimd else "passed_dve"], 1)

        def steps_of(eng, start, count, unroll, lag, step, before=None):
            before = before or (lambda i: None)
            for i in range(start):
                if i % unroll == 0:
                    before(i)
                step(i, i % unroll)
            with eng.Fori(start, count - unroll + 1, unroll) as i0:
                before(i0)
                for j in range(unroll):
                    step(i0 + j, j)
            for i in range(count, count + lag):
                if i % unroll == 0:
                    before(i)
                step(i, i % unroll)

        def read_experts(eng, experts, first):
            def read(i):
                lo, hi = first, RING - 1
                if isinstance(i, int):
                    lo, hi = max(lo, -i), min(hi, SLOTS - i)
                _, values = nc.values_load_multi_w_load_instructions(
                    eid_i[0:1, bass.ds(i + lo, hi - lo)], engines=[eng.engine], min_val=0, max_val=E - 1,
                    skip_runtime_bounds_check_because="the table is made as a minimum with E - 1")
                for q in range(lo, hi):
                    experts[q] = values[q - lo]
            return read

        def on(i, lag, count):
            return not isinstance(i, int) or 0 <= i - lag < count

        def norms(u):
            if not isinstance(u, int):
                return slice(0, 2)
            return slice(0 if u < G else 1, 2 if u >= 4 else 1)

        LAST = 8
        AHEAD = 3
        FIRST = 12

        block = ctx.enter_context(nc.Block())

        @block.sync
        def _(sp):
            def load_x(g, b):
                freed(sp, "ln1_stats", g)
                sp.dma_start(X[:, bass.ds(g * T, T), :], x_tiles[:, bass.ds(g * T, T), :]).then_inc(x_in[b], 16)

            def load_adj(g, b):
                freed(sp, "e_max", g)
                sp.dma_start(adj_sb[:, b, :, :], adj_tiles[bass.ds(g, 1)].rearrange("o p t j -> (o p) t j")
                             ).then_inc(adj_in[b], 16)

            load_x(0, 0)
            sp.dma_start(Wsb[:], W).then_inc(s["weights_in"], 16)
            sp.dma_start(a_sb[:], a.rearrange("(k o) x -> o (k x)", k=2), allow_slow_non_contiguous=True).then_inc(s["weights_in"], 16)
            load_x(1, 1)
            sp.dma_start(Wg_sb[:], Wg).then_inc(s["weights_in"], 16)
            sp.dma_start(bg_rep[:], bg.rearrange("(o e) -> o e", o=1).to_broadcast([P, E])).then_inc(s["weights_in"], 16)
            load_adj(0, 0)
            load_adj(1, 1)
            for g in range(2, AHEAD + 2):
                load_x(g, g % 2)
            sp.dma_start(W1s.rearrange("p (e h) -> p e h", e=E), W1.rearrange("e d h -> d e h")).then_inc(s["ffn_weights_in"], 16)
            sp.dma_start(W2s, W2.rearrange("e (c p) d -> p (e c) d", p=P)).then_inc(s["ffn_weights_in"], 16)
            sp.dma_start(b1_rep[:].rearrange("p e h -> p (e h)"),
                         b1.rearrange("(o e) h -> o (e h)", o=1).to_broadcast([P, E * H])).then_inc(s["ffn_weights_in"], 16)
            sp.dma_start(b2_rep[:].rearrange("p e h -> p (e h)"),
                         b2.rearrange("(o e) h -> o (e h)", o=1).to_broadcast([P, E * D])).then_inc(s["ffn_weights_in"], 16)
            whole = (G - AHEAD) // 2 * 2
            with sp.Fori(2, whole - 1, 2) as g0:
                for b in range(2):
                    load_adj(g0 + b, b)
                    load_x(g0 + b + AHEAD, (b + AHEAD) % 2)
            for g in range(whole, G):
                load_adj(g, g % 2)
                if g + AHEAD < G:
                    load_x(g + AHEAD, (g + AHEAD) % 2)

            sp.wait_ge(s["consts_made"], 1)
            for t in range(E):
                sp.dma_start(xs[E * STRIDE + t * P:E * STRIDE + (t + 1) * P, :], pad_rows[:]).then_inc(s["pads_done"], 16)
            sp.wait_ge(s["tab_ready"], 1)
            for e in range(E):
                r = sp.value_load(base_i[0:1, e:e + 1], min_val=0, max_val=E * STRIDE - P)
                sp.dma_start(xs[bass.ds(r, P), :], pad_rows[:]).then_inc(s["pads_done"], 16)
            sp.wait_ge(s["pads_done"], 16 * 2 * E)
            for b in range(RB):
                sp.wait_ge(rows_sent[b], 16 * T * K * G // RB)

            def load_tile(i, b):
                r = sp.value_load(row_i[0:1, bass.ds(i, 1)], min_val=0, max_val=XS_ROWS - P)
                if not isinstance(i, int) or i >= RING:
                    sp.wait_ge(tile_out[b], (i - b) * 2)
                sp.dma_start(xt[:, b, :], xs[bass.ds(r, P), :]).then_inc(tile_in[b], 16)

            steps_of(sp, RING, SLOTS, RING, 0, load_tile)

            for b in range(RING):
                sp.wait_ge(tile_out[b], 16 * SLOTS // RING)
            ybuf = Wstage[:].rearrange("p k (c n) -> p (k c) n", c=4)
            for c in range(NCH):
                if c >= 4:
                    sp.wait_ge(s["second_add"], c - 3)
                for k in range(K):
                    sp.dma_start(ybuf[:, (c % 4) * 2 + k, :].rearrange("p (n d) -> p n d", d=D),
                                 y_tiles[k][:, c * CH:(c + 1) * CH, :]).then_inc(y_in[c % 4], 16)
                if c >= 2:
                    sp.wait_ge(s["second_add"], c - 1)
                    sp.dma_start(out_tiles[:, (c - 2) * CH:(c - 1) * CH, :],
                                 X[:, (c - 2) * CH:(c - 1) * CH, :]).then_inc(s["stored"], 16)
            for c in range(NCH - 2, NCH):
                sp.wait_ge(s["second_add"], c + 1)
                sp.dma_start(out_tiles[:, c * CH:(c + 1) * CH, :],
                             X[:, c * CH:(c + 1) * CH, :]).then_inc(s["stored"], 16)
            sp.wait_ge(s["stored"], 16 * NCH)

        @block.gpsimd
        def _(pool):
            pool.memset(ident[:], 0.0)
            pool.memset(tri[:], 0.0)
            pool.memset(ones[:], 1.0)
            pool.memset(eps_t[:], EPS)
            pool.memset(pad_rows[:, 0:D + 1], 0.0)
            pool.memset(pad_rows[:, D + 1:D + 2].bitcast(I32), SKIP)
            pool.memset(low8[:], 0.0)
            pool.memset(rows[:], 0.0).then_inc(s["ident_zero"], 1)
            pool.wait_ge(s["ident_zero"], 1)
            pool.affine_select(out=ident[:], in_=ident[:], compare_op=ALU.not_equal, fill=1.0, base=0,
                               pattern=[[-1, P]], channel_multiplier=1)
            pool.affine_select(out=tri[:], in_=tri[:], compare_op=ALU.is_ge, fill=1.0, base=0,
                               pattern=[[-1, P]], channel_multiplier=1)
            pool.affine_select(out=low8[:], in_=low8[:], compare_op=ALU.is_gt, fill=1.0, base=0,
                               pattern=[[-1, E], [1, E]], channel_multiplier=0)
            pool.iota(iota_e[:], pattern=[[1, E]], base=0, channel_multiplier=0,
                      allow_small_or_imprecise_dtypes=True)
            pool.iota(base0[:], pattern=[[STRIDE, E]], base=0, channel_multiplier=0,
                      allow_small_or_imprecise_dtypes=True)
            pool.iota(edge[:], pattern=[[P, TILES]], base=0, channel_multiplier=0,
                      allow_small_or_imprecise_dtypes=True)
            pool.iota(tile_no[:], pattern=[[1, SLOTS]], base=0, channel_multiplier=0,
                      allow_small_or_imprecise_dtypes=True)
            pool.iota(row0[:], pattern=[[P, SLOTS]], base=0, channel_multiplier=0,
                      allow_small_or_imprecise_dtypes=True)
            pool.iota(dest[:], pattern=[[P, T], [TOK, K]], base=0, channel_multiplier=1,
                      allow_small_or_imprecise_dtypes=True).then_inc(s["consts_made"], 1)

            def send_rows(g, b):
                if not isinstance(g, int) or g >= RB:
                    pool.wait_ge(rows_sent[b], (g - b) * 16)
                if not isinstance(g, int) or g >= 1:
                    pool.wait_ge(s["dest_moved"], g)
                alone(pool)
                pool.tensor_copy(rows[:, b, :, :, D + 1].bitcast(I32), dest[:]).then_inc(s["dest_ready"], 1)
                ready(pool, "w1_hi", g)
                alone(pool)
                pool.tensor_tensor(W1lo[:, bass.ds(g * P, P)], W1s[:, bass.ds(g * P, P)],
                                   W1hi[:, bass.ds(g * P, P)].bitcast(F32), ALU.subtract).then_inc(s["w1_lo"], 1)
                ready(pool, "w2_hi", g)
                alone(pool)
                pool.tensor_tensor(W2hl[:, bass.ds(g, 1), 1, :].rearrange("p o d -> p (o d)"),
                                   W2s[:, bass.ds(g, 1), :].rearrange("p o d -> p (o d)"),
                                   W2hl[:, bass.ds(g, 1), 0, :].rearrange("p o d -> p (o d)").bitcast(F32),
                                   ALU.subtract).then_inc(s["w2_lo"], 1)
                ready(pool, "dest_ready", g)
                alone(pool)
                pool.tensor_scalar(dest[:], dest[:], float(N), None, ALU.add).then_inc(s["dest_moved"], 1)
                ready(pool, "slots_ready", g)
                alone(pool)
                for t in range(T):
                    for k in range(K):
                        pool.indirect_dma_start(xs, bass.IndirectOffsetOnAxis(ap=slot[:, b, t, k:k + 1], axis=0),
                                                rows[:, b, t, k, :], None).then_inc(rows_sent[b], 16)

            pool.wait_ge(s["consts_made"], 1)
            steps_of(pool, RB, G, RB, 0, send_rows)

            def send_tile(i, b):
                ready(pool, "y_scaled", i)
                alone(pool)
                pool.indirect_dma_start(ytok, bass.IndirectOffsetOnAxis(ap=xt[:, b, D + 1:D + 2].bitcast(I32), axis=0),
                                        ys[:, b, :], None, bounds_check=SKIP - 1, oob_is_err=False
                                        ).then_inc(tile_out[b], 16)

            steps_of(pool, RING, SLOTS, RING, 0, send_tile)

        @block.tensor
        def _(pe):
            pe.wait_ge(s["consts_made"], 1)
            pe.wait_ge(s["weights_in"], 64)
            nc.tensor.transpose(bank[0][:, 0:P], Wsb[:], ident[:]).then_inc(s["wt_ps"], 1)
            pe.wait_ge(s["wt_sb"], 1)
            nc.tensor.matmul(bank[1][:, 0:2], WT[:], a_sb[:], start=True, stop=True).then_inc(s["wa_ps"], 1)
            pe.wait_ge(s["wrep_ready"], 2)

            def transpose_xhat(g, b):
                ready(pe, "xhat_ready", g)
                freed(pe, "xhat_t_sb", g, 1)
                for t in range(T):
                    m = nc.tensor.transpose(bank[0][:, t * P:(t + 1) * P], xhat[:, b, t, :], ident[:])
                m.then_inc(s["xhat_t_ps"], 1)

            def project(g, b):
                ready(pe, "xhat_t_sb", g)
                freed(pe, "h_sb", g, 1)
                for t in range(T):
                    m = nc.tensor.matmul(bank[1][:, t * (D + 2):(t + 1) * (D + 2)], xhatT[:, b, t * P:(t + 1) * P],
                                         Waug[:], start=True, stop=True)
                m.then_inc(s["h_ps"], 1)
                freed(pe, "relu_sb", g, 1)
                nc.tensor.matmul(bank[2][:, 0:N], wa2[:], xhatT[:, b, :], start=True, stop=True).then_inc(s["dst_ps"], 1)

            def transpose_p(g, b):
                ready(pe, "p_ready", g)
                freed(pe, "p_t_sb", g, 1)
                for j in range(T):
                    for t in range(T):
                        m = nc.tensor.transpose(bank[3][:, j * N + t * P:j * N + (t + 1) * P],
                                                p_sb[:, b, t, j * P:(j + 1) * P], ident[:])
                m.then_inc(s["p_t_ps"], 1)

            def attend(g, b):
                ready(pe, "p_t_sb", g)
                freed(pe, "x1_ready", g, 1)
                for t in range(T):
                    for j in range(T):
                        m = nc.tensor.matmul(bank[4][:, t * D:(t + 1) * D], pT[:, b, j, t * P:(t + 1) * P],
                                             h_sb[:, b, j, 0:D], start=(j == 0), stop=(j == T - 1))
                m.then_inc(s["attn_ps"], 1)

            def transpose_xn(g, b, rb):
                ready(pe, "rows_ready", g)
                freed(pe, "xn_t_sb", g, 1)
                for t in range(T):
                    m = nc.tensor.transpose(bank[5][:, t * P:(t + 1) * P], rows[:, rb, t, 0, 0:D], ident[:])
                m.then_inc(s["xn_t_ps"], 1)

            def gate(g, b):
                ready(pe, "xn_t_sb", g)
                freed(pe, "logits_sb", g, 1)
                for t in range(T):
                    m = nc.tensor.matmul(bank[6][:, t * E:(t + 1) * E], xnT[:, b, t * P:(t + 1) * P], Wg_sb[:],
                                         start=True, stop=True)
                m.then_inc(s["logits_ps"], 1)

            def count(g, b):
                ready(pe, "sel_ready", g)
                freed(pe, "base_ready", g, 1)
                c = bank[7]
                nc.tensor.matmul(c[:, 0:E], tri[:], sel[:, b, 0, :], start=True, stop=True)
                nc.tensor.matmul(c[:, E:2 * E], tri[:], sel[:, b, 1, :], start=True, stop=False)
                nc.tensor.matmul(c[:, E:2 * E], ones[:], sel[:, b, 0, :], start=False, stop=True)
                nc.tensor.matmul(c[:, 2 * E:3 * E], ones[:], sel[:, b, 0, :], start=True, stop=False)
                nc.tensor.matmul(c[:, 2 * E:3 * E], ones[:], sel[:, b, 1, :], start=False, stop=True
                                 ).then_inc(s["count_ps"], 1)

            def first_layer(i, j):
                b = j % 2
                if on(i, 2, G):
                    transpose_xhat(i - 2, b)
                if on(i, 4, G):
                    transpose_p(i - 4, b)
                if on(i, 6, G):
                    transpose_xn(i - 6, b, (j - 6) % RB)
                if on(i, 4, G):
                    attend(i - 4, b)
                if on(i, 7, G):
                    count(i - 7, 1 - b)
                if on(i, 6, G):
                    gate(i - 6, b)
                if on(i, 2, G):
                    project(i - 2, b)

            steps_of(pe, FIRST, G, RB, LAST, first_layer)

            pe.wait_ge(s["tab_ready"], 1)
            pe.wait_ge(s["base_ready"], G)
            pe.wait_ge(s["w1_lo"], G)
            pe.wait_ge(s["w2_lo"], G)

            def turn_x(i, b, r):
                pe.wait_ge(tile_in[r], (i - r) * 2 + 16)
                freed(pe, "xt_lo", i)
                nc.tensor.transpose(bank[b][:, 0:P], xt[:, r, 0:D], ident[:]).then_inc(s["xt_ps"], 1)

            def up(i, b, e):
                ready(pe, "xt_lo", i)
                freed(pe, "biased", i)
                hi, lo = W1hi[:, bass.ds(e * H, H)], W1lo[:, bass.ds(e * H, H)]
                o = bank[2 + b]
                nc.tensor.matmul(o[:], xTh[:, b, :], hi, start=True, stop=False)
                nc.tensor.matmul(o[:], xTh[:, b, :], lo, start=False, stop=False)
                nc.tensor.matmul(o[:], xTl[:, b, :], hi, start=False, stop=True).then_inc(s["up_ps"], 1)

            def turn_g(i, b):
                ready(pe, "gelu_done", i)
                freed(pe, "gt_lo", i)
                for c in range(C):
                    m = nc.tensor.transpose(bank[4 + b][:, c * P:(c + 1) * P], g_sb[:, b, c * P:(c + 1) * P], ident[:])
                m.then_inc(s["gt_ps"], 1)

            def down(i, b, e):
                ready(pe, "gt_lo", i)
                freed(pe, "y_full", i)
                o = bank[6 + b]
                W2f = W2hl[:].rearrange("p b k d -> p (b k d)")
                for c in range(C):
                    nc.tensor.matmul(o[:, 0:2 * D], gTh[:, b, c * P:(c + 1) * P],
                                     W2f[:, bass.ds(e * (C * 2 * D) + c * 2 * D, 2 * D)],
                                     start=(c == 0), stop=False)
                    m = nc.tensor.matmul(o[:, 0:D], gTl[:, b, c * P:(c + 1) * P],
                                         W2f[:, bass.ds(e * (C * 2 * D) + c * 2 * D, D)],
                                         start=False, stop=(c == C - 1))
                m.then_inc(s["down_ps"], 1)

            def expert_step(i, j):
                b = j % 2
                if on(i, 0, SLOTS):
                    turn_x(i, b, j)
                if on(i, 1, SLOTS):
                    up(i - 1, 1 - b, experts[j - 1])
                if on(i, 2, SLOTS):
                    turn_g(i - 2, b)
                if on(i, 3, SLOTS):
                    down(i - 3, 1 - b, experts[j - 3])

            experts = {}
            steps_of(pe, RING, SLOTS, RING, 3, expert_step, read_experts(pe, experts, -3))

        @block.scalar
        def _(act):
            nc.scalar.preload_act_table_set("natural_log_exp_and_others")
            act.wait_ge(s["wt_ps"], 1)
            nc.scalar.activation(WT[:], bank[0][:, 0:P], ACT.Copy).then_inc(s["wt_sb"], 1)

            def roots(u, b, step):
                n = norms(u)
                if step == 0:
                    ready(act, "moments_ready", u)
                    nc.scalar.activation(root[:, b, 0, n, :], mean_var[:, b, n, :, 1], ACT.Ln, bias=eps_t[:, 0:1]
                                         ).then_inc(s["log_ready"], 1)
                else:
                    ready(act, "log_ready", u)
                    nc.scalar.activation(root[:, b, 1, n, :], root[:, b, 0, n, :], ACT.Exp, scale=-0.5
                                         ).then_inc(s["root_ready"], 1)

            def norm1(g, b):
                ready(act, "shift_ready", g)
                freed(act, "xhat_t_ps", g)
                for t in range(T):
                    m = nc.scalar.activation(xhat[:, b, t, :], X[:, bass.ds(g * T + t, 1), :].rearrange("p o d -> p (o d)"),
                                             ACT.Identity, bias=shift[:, b, t:t + 1], scale=root[:, b, 2, 0, t:t + 1])
                m.then_inc(s["xhat_ready"], 1)

            def take_scores(g, b, step):
                if step == 1:
                    ready(act, "h_sb", g)
                    for t in range(T):
                        m = nc.scalar.activation(relu_sb[:, b, t, :], bank[2][:, 0:N], ACT.Relu,
                                                 bias=h_sb[:, b, t, D:D + 1], scale=1.0 - SLOPE)
                    m.then_inc(s["relu_sb"], 1)
                    return
                ready(act, "h_ps", g)
                freed(act, "attn_ps", g)
                nc.scalar.activation(h_sb[:, b, :, :].rearrange("p t d -> p (t d)"), bank[1][:, 0:T * (D + 2)],
                                     ACT.Copy).then_inc(s["h_sb"], 1)
                ready(act, "dst_ps", g)
                freed(act, "e_sum", g)
                nc.scalar.activation(dst_sb[:, b, :], bank[2][:, 0:N], ACT.Copy, scale=SLOPE).then_inc(s["dst_sb"], 1)

            def exps(g, b, t):
                if t == 0:
                    ready(act, "negmax_ready", g)
                    freed(act, "p_t_ps", g)
                    freed(act, "rinv_ready", g)
                m = nc.scalar.activation(p_sb[:, b, t, :], e_sb[:, b, t, :], ACT.Exp, bias=nmax[:, b, t:t + 1],
                                         accum_out=psums[:, b, t:t + 1])
                if t == T - 1:
                    m.then_inc(s["p_ready"], 1)

            def copy_out(g, b, ps, dst, src, done, user):
                ready(act, ps, g)
                freed(act, user, g)
                nc.scalar.activation(dst, src, ACT.Copy).then_inc(s[done], 1)

            def gate_exp(g, b):
                ready(act, "gap_ready", g)
                nc.scalar.activation(gap[:, b, 1, :], gap[:, b, 0, :], ACT.Exp).then_inc(s["gap_exp"], 1)

            def split_weights(g):
                if isinstance(g, int) and g == 0:
                    act.wait_ge(s["ffn_weights_in"], 64)
                nc.scalar.activation(W1hi[:, bass.ds(g * P, P)], W1s[:, bass.ds(g * P, P)], ACT.Copy
                                     ).then_inc(s["w1_hi"], 1)
                nc.scalar.activation(W2hl[:, bass.ds(g, 1), 0, :].rearrange("p o d -> p (o d)"),
                                     W2s[:, bass.ds(g, 1), :].rearrange("p o d -> p (o d)"), ACT.Copy
                                     ).then_inc(s["w2_hi"], 1)

            def first_layer(i, j):
                b = j % 2
                c = 1 - b
                if on(i, 1, G + 4):
                    roots(i - 1, c, 0)
                if on(i, 3, G):
                    take_scores(i - 3, c, 0)
                if on(i, 1, G + 4):
                    roots(i - 1, c, 1)
                if on(i, 3, G):
                    take_scores(i - 3, c, 1)
                if on(i, 2, G):
                    copy_out(i - 2, b, "xhat_t_ps", xhatT[:, b, :], bank[0][:, 0:N], "xhat_t_sb", "dst_ps")
                if on(i, 4, G):
                    copy_out(i - 4, b, "p_t_ps", pT[:, b, :, :].rearrange("p j n -> p (j n)"), bank[3][:],
                             "p_t_sb", "attn_ps")
                if on(i, 6, G):
                    copy_out(i - 6, b, "xn_t_ps", xnT[:, b, :], bank[5][:, 0:N], "xn_t_sb", "logits_ps")
                if on(i, 7, G):
                    gate_exp(i - 7, c)
                if on(i, 5, G):
                    split_weights(i - 5)
                if on(i, 1, G):
                    norm1(i - 1, c)
                if on(i, 3, G):
                    exps(i - 3, c, 0)
                    exps(i - 3, c, 1)

            steps_of(act, FIRST, G, 2, LAST, first_layer)

            def expert_step(i, j):
                b = j % 2
                if on(i, 0, SLOTS):
                    ready(act, "xt_ps", i)
                    freed(act, "up_ps", i)
                    nc.scalar.activation(xTh[:, b, :], bank[b][:, 0:P], ACT.Copy).then_inc(s["xt_hi"], 1)
                if on(i, 5, SLOTS):
                    n, r = i - 5, (j - 5) % RING
                    ready(act, "y_full", n)
                    if isinstance(i, int):
                        if n >= RING:
                            act.wait_ge(tile_out[r], n // RING * 16)
                    else:
                        act.wait_ge(tile_out[r], (i - j) * 2 - (0 if j >= 5 else 16))
                    nc.scalar.activation(ys[:, r, :], yb[:, 1 - b, :], ACT.Copy, scale=xt[:, r, D:D + 1]
                                         ).then_inc(s["y_scaled"], 1)
                if on(i, 2, SLOTS):
                    ready(act, "gt_ps", i - 2)
                    freed(act, "down_ps", i - 2)
                    nc.scalar.activation(gTh[:, b, :], bank[4 + b][:], ACT.Copy).then_inc(s["gt_hi"], 1)
                if on(i, 1, SLOTS):
                    ready(act, "biased", i - 1)
                    freed(act, "gt_ps", i - 1)
                    nc.scalar.activation(g_sb[:, 1 - b, :], hb[:, 1 - b, :], ACT.Gelu).then_inc(s["gelu_done"], 1)

            steps_of(act, 2 * RING, SLOTS, RING, 5, expert_step)

        @block.vector
        def _(dve):
            dve.wait_ge(s["consts_made"], 1)
            dve.tensor_copy(base[:], base0[:]).then_inc(s["base_init"], 1)
            dve.wait_ge(s["wa_ps"], 1)
            dve.tensor_scalar(Waug[:, D:D + 2], bank[1][:, 0:2], 1.0 - SLOPE, None, ALU.mult).then_inc(s["wrep_ready"], 1)
            dve.tensor_copy(Waug[:, 0:D], Wsb[:]).then_inc(s["wa_sb"], 1)
            dve.tensor_copy(wa2[:], bank[1][:, 1:2].to_broadcast([P, P])).then_inc(s["wrep_ready"], 1)
            dve.wait_ge(s["wa_sb"], 1)
            dve.wait_ge(s["base_init"], 1)

            def xg(g, t):
                return X[:, bass.ds(g * T + t, 1), :].rearrange("p o d -> p (o d)")

            def stats(g, b, norm, done, t):
                m = dve.bn_stats(stat[:, b, norm, t, :], xg(g, t))
                if t == T - 1:
                    m.then_inc(s[done], 1)

            def moments(i, b):
                n = norms(i)
                if n.start == 0:
                    ready(dve, "ln1_stats", i)
                if n.stop == 2:
                    ready(dve, "ln2_stats", i - 4)
                alone(dve)
                for q in range(n.start, n.stop):
                    for t in range(T):
                        m = dve.bn_aggr(mean_var[:, b, q, t, :], stat[:, b, q, t, :])
                m.then_inc(s["moments_ready"], 1)

            def newton(u, b, step):
                n = norms(u)
                src, dst, num, op, done, wait = [
                    (mean_var[:, b, n, :, 1], 2, EPS, ALU.add, "newton1", "root_ready"),
                    (root[:, b, 2, n, :], 3, -0.5, ALU.mult, "newton2", "newton1"),
                    (root[:, b, 3, n, :], 2, 1.5, ALU.add, "rstd_ready", "newton2")][step]
                ready(dve, wait, u)
                dve.scalar_tensor_tensor(out=root[:, b, dst, n, :], in0=src, scalar=num, in1=root[:, b, 1, n, :],
                                         op0=op, op1=ALU.mult).then_inc(s[done], 1)

            def make_shift(g, b):
                ready(dve, "rstd_ready", g)
                dve.scalar_tensor_tensor(out=shift[:, b, :], in0=mean_var[:, b, 0, :, 0], scalar=-1.0,
                                         in1=root[:, b, 2, 0, :], op0=ALU.mult, op1=ALU.mult
                                         ).then_inc(s["shift_ready"], 1)

            def norm2(g, rb, t, u):
                if t == 0:
                    ready(dve, "rstd_ready", g + 4)
                    if not isinstance(g, int) or g >= RB:
                        dve.wait_ge(rows_sent[rb], (g - rb) * 16)
                m = dve.tensor_scalar(rows[:, rb, t, :, 0:D], X[:, bass.ds(g * T + t, 1), :].to_broadcast([P, K, D]),
                                      mean_var[:, u, 1, t, 0:1], root[:, u, 2, 1, t:t + 1], ALU.subtract, ALU.mult)
                if t == T - 1:
                    m.then_inc(s["rows_ready"], 1)

            def make_mask(g, b):
                dve.wait_ge(adj_in[b], (g - b) * 8 + 16)
                dve.tensor_scalar(adj_sb[:, b, :, :], adj_sb[:, b, :, :], 0.0, NEG, ALU.is_le, ALU.mult
                                  ).then_inc(s["mask_ready"], 1)

            def sum_scores(g, b):
                ready(dve, "relu_sb", g)
                freed(dve, "p_ready", g)
                dve.tensor_tensor(e_sb[:, b, :, :], relu_sb[:, b, :, :],
                                  dst_sb[:, b, :].rearrange("p (x n) -> p x n", x=1).to_broadcast([P, T, N]), ALU.add
                                  ).then_inc(s["e_sum"], 1)

            def mask_scores(g, b):
                ready(dve, "e_sum", g)
                ready(dve, "mask_ready", g)
                alone(dve)
                for t in range(T):
                    m = dve.tensor_tensor_reduce(e_sb[:, b, t, :], e_sb[:, b, t, :], adj_sb[:, b, t, :], 1.0, -3.0e38,
                                                 ALU.add, ALU.max, emax[:, b, t:t + 1])
                m.then_inc(s["e_max"], 1)

            def negate_max(g, b):
                ready(dve, "e_max", g)
                dve.tensor_scalar(nmax[:, b, :], emax[:, b, :], -1.0, None, ALU.mult).then_inc(s["negmax_ready"], 1)

            def invert_sums(g, b):
                ready(dve, "p_ready", g)
                dve.reciprocal(rinv[:, b, :], psums[:, b, :]).then_inc(s["rinv_ready"], 1)

            def residual(g, b, t):
                if t == 0:
                    ready(dve, "rinv_ready", g)
                    ready(dve, "attn_ps", g)
                m = dve.scalar_tensor_tensor(out=xg(g, t), in0=bank[4][:, t * D:(t + 1) * D],
                                             scalar=rinv[:, b, t:t + 1], in1=xg(g, t), op0=ALU.mult, op1=ALU.add)
                if t == T - 1:
                    m.then_inc(s["x1_ready"], 1)

            def add_gate_bias(g, b):
                ready(dve, "logits_ps", g)
                dve.tensor_tensor(lg[:, b, :, :], bank[6][:, 0:T * E].rearrange("p (t e) -> p t e", t=T),
                                  bg_rep[:].rearrange("p (x e) -> p x e", x=1).to_broadcast([P, T, E]), ALU.add
                                  ).then_inc(s["logits_sb"], 1)

            def top_values(g, b):
                ready(dve, "logits_sb", g)
                alone(dve)
                for t in range(T):
                    m = dve.max(top[:, b, t, :], lg[:, b, t, :])
                m.then_inc(s["top_ready"], 1)

            def top_indices(g, b):
                ready(dve, "top_ready", g)
                alone(dve)
                dve.tensor_tensor(gap[:, b, 0, :], top[:, b, :, 1], top[:, b, :, 0], ALU.subtract
                                  ).then_inc(s["gap_ready"], 1)
                for t in range(T):
                    m = dve.max_index(topi[:, b, t, :], top[:, b, t, :], lg[:, b, t, :])
                m.then_inc(s["index_ready"], 1)

            def copy_picks(g, b):
                ready(dve, "index_ready", g)
                dve.tensor_copy(pick[:, b, :, :], topi[:, b, :, 0:K]).then_inc(s["picks_ready"], 1)

            def one_hot(g, b):
                ready(dve, "picks_ready", g)
                dve.tensor_tensor(hot[:, b, :, :, :].rearrange("p t k e -> p (t k) e"),
                                  iota_e[:].rearrange("p (x e) -> p x e", x=1).to_broadcast([P, T * K, E]),
                                  pick[:, b, :, :].rearrange("p t (k x) -> p (t k) x", x=1).to_broadcast([P, T * K, E]),
                                  ALU.is_equal).then_inc(s["onehot_ready"], 1)

            def select(g, b):
                ready(dve, "onehot_ready", g)
                freed(dve, "count_ps", g)
                dve.tensor_tensor(sel[:, b, :, :], hot[:, b, :, 0, :], hot[:, b, :, 1, :], ALU.add
                                  ).then_inc(s["sel_ready"], 1)

            def gates(g, b, rb, step):
                if step == 0:
                    ready(dve, "gap_exp", g)
                    dve.tensor_scalar(gap[:, b, 2, :], gap[:, b, 1, :], 1.0, None, ALU.add).then_inc(s["gate_den"], 1)
                if step == 1:
                    ready(dve, "gate_den", g)
                    dve.reciprocal(rows[:, rb, :, 0, D], gap[:, b, 2, :]).then_inc(s["gate_first"], 1)
                if step == 2:
                    ready(dve, "gate_first", g)
                    dve.tensor_tensor(rows[:, rb, :, 1, D], rows[:, rb, :, 0, D], gap[:, b, 1, :], ALU.mult
                                      ).then_inc(s["gates_ready"], 1)

            def place(g, b, rb, step):
                if step == 0:
                    ready(dve, "count_ps", g)
                    if not isinstance(g, int) or g >= 1:
                        dve.wait_ge(s["base_ready"], g)
                    dve.tensor_tensor(pos[:, b, :, :], bank[7][:, 0:T * E].rearrange("p (t e) -> p t e", t=T),
                                      base[:].rearrange("p (x e) -> p x e", x=1).to_broadcast([P, T, E]), ALU.add
                                      ).then_inc(s["pos_ready"], 1)
                if step == 1:
                    ready(dve, "pos_ready", g)
                    dve.tensor_tensor(base[:], bank[7][:, 2 * E:3 * E], base[:], ALU.add).then_inc(s["base_ready"], 1)
                    for t in range(T):
                        m = dve.tensor_tensor(posm[:, b, t, :, :], hot[:, b, t, :, :],
                                              pos[:, b, t:t + 1, :].to_broadcast([P, K, E]), ALU.mult)
                    m.then_inc(s["posmask_ready"], 1)
                if step == 2:
                    ready(dve, "posmask_ready", g)
                    ready(dve, "gates_ready", g)
                    with nc.allow_low_precision(reason="a sum of one row number and zeros, all whole"):
                        dve.tensor_reduce(slot[:, rb, :, :], posm[:, b, :, :, :], AX.X, ALU.add
                                          ).then_inc(s["slots_ready"], 1)

            def first_layer(i, j):
                b = j % 2
                c = 1 - b
                r6, r7, r8 = (j - 6) % RB, (j - 7) % RB, j % RB
                roots_on, norm_on, score_on, sum_on = on(i, 1, G + 4), on(i, 1, G), on(i, 3, G), on(i, 4, G)
                row_on, route_on, place_on = on(i, 6, G), on(i, 7, G), on(i, 8, G)
                if score_on:
                    make_mask(i - 3, c)
                if route_on:
                    add_gate_bias(i - 7, c)
                if row_on:
                    norm2(i - 6, r6, 0, b)
                if route_on:
                    top_values(i - 7, c)
                if row_on:
                    norm2(i - 6, r6, 1, b)
                if route_on:
                    top_indices(i - 7, c)
                if place_on:
                    place(i - 8, b, r8, 0)
                if roots_on:
                    newton(i - 1, c, 0)
                if route_on:
                    copy_picks(i - 7, c)
                if place_on:
                    place(i - 8, b, r8, 1)
                if roots_on:
                    newton(i - 1, c, 1)
                if route_on:
                    one_hot(i - 7, c)
                if score_on:
                    sum_scores(i - 3, c)
                if roots_on:
                    newton(i - 1, c, 2)
                if route_on:
                    select(i - 7, c)
                if place_on:
                    place(i - 8, b, r8, 2)
                if norm_on:
                    make_shift(i - 1, c)
                if score_on:
                    mask_scores(i - 3, c)
                if on(i, 0, G):
                    dve.wait_ge(x_in[b], (i - b) * 8 + 16)
                    alone(dve)
                    stats(i, b, 0, "ln1_stats", 0)
                if score_on:
                    negate_max(i - 3, c)
                if on(i, 0, G):
                    stats(i, b, 0, "ln1_stats", 1)
                if route_on:
                    gates(i - 7, c, r7, 0)
                if sum_on:
                    invert_sums(i - 4, b)
                if route_on:
                    gates(i - 7, c, r7, 1)
                if sum_on:
                    residual(i - 4, b, 0)
                if route_on:
                    gates(i - 7, c, r7, 2)
                if sum_on:
                    residual(i - 4, b, 1)
                    ready(dve, "x1_ready", i - 4)
                    alone(dve)
                    stats(i - 4, b, 1, "ln2_stats", 0)
                    stats(i - 4, b, 1, "ln2_stats", 1)
                if on(i, 0, G + 4):
                    moments(i, b)

            steps_of(dve, FIRST, G, RB, LAST, first_layer)

            dve.wait_ge(s["base_ready"], G)
            dve.tensor_tensor(cnt[:], base[0:1, :], base0[0:1, :], ALU.subtract).then_inc(s["cnt_ready"], 1)
            dve.tensor_copy(base_i[:], base[0:1, :]).then_inc(s["tab_f"], 1)
            dve.wait_ge(s["cnt_ready"], 1)
            dve.tensor_tensor(over[:], cnt[:].rearrange("o (e x) -> o e x", x=1).to_broadcast([1, E, TILES]),
                              edge[:].rearrange("o (x n) -> o x n", x=1).to_broadcast([1, E, TILES]),
                              ALU.is_gt).then_inc(s["over_ready"], 1)
            dve.wait_ge(s["over_ready"], 1)
            dve.tensor_reduce(ntile[:], over[:], AX.X, ALU.add).then_inc(s["ntile_ready"], 1)
            dve.wait_ge(s["ntile_ready"], 1)
            dve.tensor_tensor(ntri[:], low8[:], ntile[:].rearrange("o (x e) -> o x e", x=1).to_broadcast([1, E, E]),
                              ALU.mult).then_inc(s["ntri_ready"], 1)
            dve.tensor_scalar(span[:], ntile[:], -float(P), float(STRIDE), ALU.mult, ALU.add
                              ).then_inc(s["span_ready"], 1)
            dve.wait_ge(s["ntri_ready"], 1)
            dve.tensor_reduce(cumend[:], ntri[:], AX.X, ALU.add).then_inc(s["cumend_ready"], 1)
            dve.wait_ge(s["cumend_ready"], 1)
            dve.tensor_tensor(comp[:], tile_no[:].rearrange("o (n x) -> o n x", x=1).to_broadcast([1, SLOTS, E]),
                              cumend[:].rearrange("o (x e) -> o x e", x=1).to_broadcast([1, SLOTS, E]),
                              ALU.is_ge).then_inc(s["comp_ready"], 1)
            dve.wait_ge(s["comp_ready"], 1)
            dve.wait_ge(s["span_ready"], 1)
            dve.tensor_reduce(eid[:], comp[:], AX.X, ALU.add).then_inc(s["eid_ready"], 1)
            dve.tensor_tensor(compm[:], comp[:], span[:].rearrange("o (x e) -> o x e", x=1).to_broadcast([1, SLOTS, E]),
                              ALU.mult).then_inc(s["spanmul_ready"], 1)
            dve.wait_ge(s["spanmul_ready"], 1)
            dve.tensor_reduce(rowsum[:], compm[:], AX.X, ALU.add).then_inc(s["rowsum_ready"], 1)
            dve.wait_ge(s["eid_ready"], 1)
            dve.tensor_scalar(eid_i[:, 0:SLOTS], eid[:], float(E - 1), None, ALU.min).then_inc(s["tab_f"], 1)
            dve.wait_ge(s["rowsum_ready"], 1)
            dve.tensor_tensor(row_i[:, 0:SLOTS], rowsum[:], row0[:], ALU.add).then_inc(s["tab_f"], 1)
            dve.wait_ge(s["tab_f"], 3)
            dve.nop().then_inc(s["tab_ready"], 1)

            def expert_step(i, j):
                b = j % 2
                if on(i, 3, SLOTS):
                    ready(dve, "gt_hi", i - 3)
                    dve.tensor_tensor(gTl[:, 1 - b, :], bank[5 - b][:], gTh[:, 1 - b, :].bitcast(F32), ALU.subtract
                                      ).then_inc(s["gt_lo"], 1)
                if on(i, 0, SLOTS):
                    ready(dve, "xt_hi", i)
                    dve.tensor_tensor(xTl[:, b, :], bank[b][:, 0:P], xTh[:, b, :].bitcast(F32), ALU.subtract
                                      ).then_inc(s["xt_lo"], 1)
                if on(i, 1, SLOTS):
                    n, q, e = i - 1, 1 - b, experts[j - 1]
                    ready(dve, "up_ps", n)
                    freed(dve, "gelu_done", n)
                    dve.tensor_tensor(hb[:, q, :], bank[2 + q][:],
                                      b1_rep[:, bass.ds(e, 1), :].rearrange("p o h -> p (o h)"), ALU.add
                                      ).then_inc(s["biased"], 1)
                if on(i, 4, SLOTS):
                    n, e = i - 4, experts[j - 4]
                    ready(dve, "down_ps", n)
                    dve.tensor_tensor(ya[:, b, :], bank[6 + b][:, 0:D],
                                      b2_rep[:, bass.ds(e, 1), :].rearrange("p o h -> p (o h)"), ALU.add
                                      ).then_inc(s["y_half"], 1)
                    ready(dve, "y_half", n)
                    freed(dve, "y_scaled", n)
                    dve.tensor_tensor(yb[:, b, :], bank[6 + b][:, D:2 * D], ya[:, b, :], ALU.add
                                      ).then_inc(s["y_full"], 1)

            experts = {}
            steps_of(dve, RING, SLOTS, RING, 4, expert_step, read_experts(dve, experts, -4))

            ybuf = Wstage[:].rearrange("p k (c n) -> p (k c) n", c=4)
            for c in range(NCH):
                xc = X[:, c * CH:(c + 1) * CH, :].rearrange("p n d -> p (n d)")
                dve.wait_ge(y_in[c % 4], 32 * (c // 4 + 1))
                dve.tensor_tensor(xc, xc, ybuf[:, (c % 4) * 2, :], ALU.add).then_inc(s["first_add"], 1)
                dve.wait_ge(s["first_add"], c + 1)
                dve.tensor_tensor(xc, xc, ybuf[:, (c % 4) * 2 + 1, :], ALU.add).then_inc(s["second_add"], 1)


_INS = ['x', 'adj', 'L0_gnn_W', 'L0_gnn_a', 'L0_ffn_Wg', 'L0_ffn_bg', 'L0_ffn_W1', 'L0_ffn_b1', 'L0_ffn_W2', 'L0_ffn_b2']


def kernel(**inputs):
    import numpy as _np
    import concourse.bacc as _bacc
    from concourse import mybir as _mybir
    from concourse.bass_utils import run_bass_kernel_spmd as _run

    nc = _bacc.Bacc("TRN2", target_bir_lowering=False, num_devices=1)
    arrays, args = {}, []
    for name in _INS:
        v = _np.ascontiguousarray(inputs[name])
        arrays[f"in_{name}_dram"] = v
        args.append(nc.dram_tensor(f"in_{name}_dram", v.shape, _mybir.dt.from_np(v.dtype), kind="ExternalInput").ap())
    args.append(nc.dram_tensor("out_dram", (G, N, D), _mybir.dt.float32, kind="ExternalOutput").ap())
    build(nc, *args)
    r = _run(nc, [arrays], core_ids=[0])
    return r.results[0]["out_dram"]
```

```python
from contextlib import ExitStack

import concourse.bass as bass
from concourse import mybir

F32 = mybir.dt.float32
F32R = mybir.dt.float32r
BF16 = mybir.dt.bfloat16
I32 = mybir.dt.int32
U32 = mybir.dt.uint32
ALU = mybir.AluOpType
ACT = mybir.ActivationFunctionType
AX = mybir.AxisListType

P = 128
G, N, D = 32, 256, 128
T = N // P
E, H, K = 8, 512, 2
C = H // P
TOK = G * N
TILES = TOK // P
ROW = D + 2
STRIDE = TOK + P
SLOTS = TOK * K // P + E
PAD_ROWS = E * P
XS_ROWS = E * STRIDE + PAD_ROWS
SKIP = TOK * K
NEG = -9000000000000000.0
SLOPE = 0.2
EPS = 1e-5
RB = 4
RING = 8
CH = 8
NCH = TILES // CH

SEMAPHORES = """
    consts_made ident_zero small_in biases_in wt_ps wt_sb wa_ps wa_sb wrep_ready
    ln1_stats ln2_stats moments_ready log_ready root_ready newton1 newton2 rstd_ready
    shift_ready xhat_ready xhat_t_ps xhat_t_sb h_ps dst_ps h_sb dst_sb relu_sb
    mask_ready e_max negmax_ready p_ready rinv_ready p_t_ps p_t_sb attn_ps
    x1_ready rows_ready
    xn_t_ps xn_t_sb logits_ps logits_sb top_ready index_ready picks_ready gap_ready gap_exp
    gate_den gate_first gates_ready onehot_ready sel_ready count_ps pos_ready posmask_ready
    slots_ready base_ready dest_ready dest_moved base_init
    w1_hi w2_hi w1_lo w2_lo
    ends_ready over_ready ntile_ps ntile_ready weigh_ready cumend_ps cumend_ready past_ready sums_ps
    tab_ready pads_done
    xt_ps xt_hi xt_lo up_ps biased gelu_done gt_ps gt_hi gt_lo down_ps y_half y_full y_scaled
    first_add second_add stored passed_pool passed_dve
""".split()


def build(nc, x, adj, W, a, Wg, bg, W1, b1, W2, b2, out):
    xs = nc.dram_tensor("routed_rows", (XS_ROWS, ROW), F32, kind="Internal").ap()
    ytok = nc.dram_tensor("expert_out", (K * TOK, D), F32, kind="Internal").ap()
    x_tiles = x.rearrange("g (t p) d -> p (g t) d", p=P)
    out_tiles = out.rearrange("g (t p) d -> p (g t) d", p=P)
    adj_tiles = adj.rearrange("g (t p) j -> g p t j", p=P)
    W2_chunks = W2.rearrange("e (c p) d -> p (e c) d", p=P)
    y_tiles = ytok.rearrange("(k n p) d -> k p n d", k=K, p=P)

    with ExitStack() as ctx:
        def sb(name, shape, dt=F32):
            return ctx.enter_context(nc.sbuf_tensor(name, shape, dt))

        s = {n: ctx.enter_context(nc.semaphore(n)) for n in SEMAPHORES}
        x_in = [ctx.enter_context(nc.semaphore(f"x_in{i}")) for i in range(2)]
        adj_in = [ctx.enter_context(nc.semaphore(f"adj_in{i}")) for i in range(2)]
        weights_in = [ctx.enter_context(nc.semaphore(f"weights_in{i}")) for i in range(C)]
        rows_sent = [ctx.enter_context(nc.semaphore(f"rows_sent{i}")) for i in range(RB)]
        tile_in = [ctx.enter_context(nc.semaphore(f"tile_in{i}")) for i in range(RING)]
        tile_out = [ctx.enter_context(nc.semaphore(f"tile_out{i}")) for i in range(RING)]
        y_in = [ctx.enter_context(nc.semaphore(f"y_in{i}")) for i in range(4)]

        bank = [ctx.enter_context(nc.psum_tensor(f"bank{i}", [P, 512], F32)) for i in range(8)]

        X = sb("X", [P, TILES, D])
        ident = sb("ident", [P, P])
        ident16 = sb("ident16", [P, P], BF16)
        tri = sb("tri", [P, P], BF16)
        ones = sb("ones", [P, P], BF16)
        iota_e = sb("iota_e", [P, E])
        Waug = sb("Waug", [P, D + 1])
        Wsb = sb("Wsb", [P, D])
        WT = sb("WT", [P, P])
        a_sb = sb("a_sb", [P, 2])
        wa2 = sb("wa2", [P, P])
        Wg_sb = sb("Wg_sb", [P, E])
        bg_rep = sb("bg_rep", [P, E])
        b1_rep = sb("b1_rep", [P, E, H])
        b2_rep = sb("b2_rep", [P, E, D])
        Wstage = sb("Wstage", [P, 2, E * H])
        W1hi = sb("W1hi", [P, E * H], F32R)
        W1lo = sb("W1lo", [P, E * H], F32R)
        W2hl = sb("W2hl", [P, E * C, 2, D], F32R)
        W1s = Wstage[:, 0, :]
        W2s = Wstage[:, 1, :].rearrange("p (b d) -> p b d", d=D)

        adj_sb = sb("adj_sb", [P, 2, T, N])
        stat = sb("stat", [P, 2, 2, T, 6])
        mean_var = sb("mean_var", [P, 2, 2, T, 2])
        root = sb("root", [P, 2, 4, 2, T])
        shift = sb("shift", [P, 2, T])
        xhat = sb("xhat", [P, 2, T, D])
        xhatT = sb("xhatT", [P, 2, N])
        h_sb = sb("h_sb", [P, 2, T, D + 1])
        dst_sb = sb("dst_sb", [P, 2, T, N])
        relu_sb = sb("relu_sb", [P, 2, T, N])
        mask = sb("mask", [P, 2, T, N], BF16)
        emax = sb("emax", [P, 2, T])
        nmax = sb("nmax", [P, 2, T])
        p_sb = sb("p_sb", [P, 2, T, N])
        psums = sb("psums", [P, 2, T])
        rinv = sb("rinv", [P, 2, T])
        pT = sb("pT", [P, 2, T, N])
        rows = sb("rows", [P, RB, T, K, ROW])
        xnT = sb("xnT", [P, 2, N])
        lg = sb("lg", [P, 2, T, E])
        top = sb("top", [P, 2, T, 8])
        topi = sb("topi", [P, 2, T, 8], U32)
        pick = sb("pick", [P, 2, T, K])
        gap = sb("gap", [P, 2, 4, T])
        hot = sb("hot", [P, 2, T, K, E])
        sel = sb("sel", [P, 2, T, E], BF16)
        pos = sb("pos", [P, 2, T, E])
        posm = sb("posm", [P, 2, T, K, E])
        slot = sb("slot", [P, RB, T, K], I32)
        base = sb("base", [P, E])
        base0 = sb("base0", [P, E])
        dest = sb("dest", [P, T, K])
        eps_t = sb("eps_t", [P, 1])

        edge = sb("edge", [P, 1])
        upto = sb("upto", [E, E])
        over = sb("over", [P, E], BF16)
        ntile = sb("ntile", [E, 1])
        cumend = sb("cumend", [E, 1])
        weigh = sb("weigh", [E, 2])
        tile_no = sb("tile_no", [E, SLOTS])
        past = sb("past", [E, SLOTS])
        row0 = sb("row0", [1, SLOTS])
        eid_i = sb("eid_i", [1, SLOTS + 8], I32)
        row_i = sb("row_i", [1, SLOTS + 8], I32)
        base_i = sb("base_i", [1, E], I32)
        pad_rows = sb("pad_rows", [P, ROW])

        spare = Wstage[:].rearrange("p k n -> p (k n)")
        taken = [0]

        def part(*shape):
            n = 1
            for d in shape:
                n *= d
            taken[0] += n
            names = "abc"[:len(shape)]
            return spare[:, taken[0] - n:taken[0]].rearrange(
                f"p ({' '.join(names)}) -> p {' '.join(names)}", **dict(zip(names, shape)))

        xt = part(RING, ROW)
        xTh = sb("xTh", [P, 2, P], F32R)
        xTl = sb("xTl", [P, 2, P], F32R)
        hb = part(2, H)
        g_sb = part(2, H)
        gTh = sb("gTh", [P, 2, H], F32R)
        gTl = sb("gTl", [P, 2, H], F32R)
        ya = part(2, D)
        yb = part(2, D)
        ys = part(RING, D)

        def ready(eng, name, g):
            eng.wait_ge(s[name], g + 1)

        def freed(eng, name, g, depth=2):
            if not isinstance(g, int) or g >= depth:
                eng.wait_ge(s[name], g + 1 - depth)

        def alone(eng):
            eng.sem_inc(s["passed_pool" if eng is nc.gpsimd else "passed_dve"], 1)

        def steps_of(eng, start, count, unroll, lag, step, before=None):
            before = before or (lambda i: None)
            for i in range(start):
                if i % unroll == 0:
                    before(i)
                step(i, i % unroll)
            with eng.Fori(start, count - unroll + 1, unroll) as i0:
                before(i0)
                for j in range(unroll):
                    step(i0 + j, j)
            for i in range(count, count + lag):
                if i % unroll == 0:
                    before(i)
                step(i, i % unroll)

        def read_experts(eng, experts, first):
            def read(i):
                lo, hi = first, RING - 1
                if isinstance(i, int):
                    lo, hi = max(lo, -i), min(hi, SLOTS - i)
                _, values = nc.values_load_multi_w_load_instructions(
                    eid_i[0:1, bass.ds(i + lo, hi - lo)], engines=[eng.engine], min_val=0, max_val=E - 1,
                    skip_runtime_bounds_check_because="the table is made as a minimum with E - 1")
                for q in range(lo, hi):
                    experts[q] = values[q - lo]
            return read

        def on(i, lag, count):
            return not isinstance(i, int) or 0 <= i - lag < count

        def norms(u):
            if not isinstance(u, int):
                return slice(0, 2)
            return slice(0 if u < G else 1, 2 if u >= 4 else 1)

        LAST = 8
        FIRST = 12

        block = ctx.enter_context(nc.Block())

        @block.sync
        def _(sp):
            def load_x(g, b):
                freed(sp, "ln1_stats", g)
                sp.dma_start(X[:, bass.ds(g * T, T), :], x_tiles[:, bass.ds(g * T, T), :]).then_inc(x_in[b], 16)

            def load_adj(g, b):
                freed(sp, "mask_ready", g)
                sp.dma_start(adj_sb[:, b, :, :], adj_tiles[bass.ds(g, 1)].rearrange("o p t j -> (o p) t j")
                             ).then_inc(adj_in[b], 16)

            def load_weights(g, e, c):
                freed(sp, "w2_hi", g, C)
                sp.dma_start(W1s[:, bass.ds(g * P, P)],
                             W1[bass.ds(e, 1), :, c * P:(c + 1) * P].rearrange("o d h -> (o d) h")
                             ).then_inc(weights_in[c], 16)
                sp.dma_start(W2s[:, bass.ds(g, 1), :], W2_chunks[:, bass.ds(g, 1), :]).then_inc(weights_in[c], 16)

            load_x(0, 0)
            sp.dma_start(Wsb[:], W).then_inc(s["small_in"], 16)
            sp.dma_start(a_sb[:], a.rearrange("(k o) x -> o (k x)", k=2), allow_slow_non_contiguous=True).then_inc(s["small_in"], 16)
            load_x(1, 1)
            sp.dma_start(Wg_sb[:], Wg).then_inc(s["small_in"], 16)
            sp.dma_start(bg_rep[:], bg.rearrange("(o e) -> o e", o=1).to_broadcast([P, E])).then_inc(s["small_in"], 16)

            def load_graph(g, e, c):
                load_adj(g, c % 2)
                if not isinstance(g, int) or g >= 1 and g + 1 < G:
                    load_x(g + 1, (c + 1) % 2)
                load_weights(g, e, c)

            for g in range(C):
                load_graph(g, 0, g)
            assert G == E * C
            with sp.Fori(1, E - 1) as e:
                for c in range(C):
                    load_graph(e * C + c, e, c)
            for g in range(G - C, G):
                load_graph(g, E - 1, g % C)
            sp.dma_start(b1_rep[:].rearrange("p e h -> p (e h)"),
                         b1.rearrange("(o e) h -> o (e h)", o=1).to_broadcast([P, E * H])).then_inc(s["biases_in"], 16)
            sp.dma_start(b2_rep[:].rearrange("p e h -> p (e h)"),
                         b2.rearrange("(o e) h -> o (e h)", o=1).to_broadcast([P, E * D])).then_inc(s["biases_in"], 16)

            sp.wait_ge(s["consts_made"], 1)
            for t in range(E):
                sp.dma_start(xs[E * STRIDE + t * P:E * STRIDE + (t + 1) * P, :], pad_rows[:]).then_inc(s["pads_done"], 16)
            sp.wait_ge(s["ends_ready"], 1)
            _, ends = nc.values_load_multi_w_load_instructions(
                base_i[0:1, :], engines=[sp.engine], min_val=0, max_val=E * STRIDE - P,
                skip_runtime_bounds_check_because="a region has room for every token and these rows")
            for e in range(E):
                sp.dma_start(xs[bass.ds(ends[e], P), :], pad_rows[:]).then_inc(s["pads_done"], 16)
            sp.wait_ge(s["tab_ready"], 2)
            sp.wait_ge(s["pads_done"], 16 * 2 * E)
            for b in range(RB):
                sp.wait_ge(rows_sent[b], 16 * T * K * G // RB)

            def load_tile(i, b):
                r = nc.values_load(row_i[0:1, bass.ds(i, 1)], engines=[sp.engine], min_val=0, max_val=XS_ROWS - P,
                                   skip_runtime_bounds_check_because="made from whole tiles of the regions")
                if not isinstance(i, int) or i >= RING:
                    sp.wait_ge(tile_out[b], (i - b) * 2)
                sp.dma_start(xt[:, b, :], xs[bass.ds(r, P), :]).then_inc(tile_in[b], 16)

            steps_of(sp, RING, SLOTS, RING, 0, load_tile)

            for b in range(RING):
                sp.wait_ge(tile_out[b], 16 * SLOTS // RING)
            ybuf = Wstage[:].rearrange("p k (c n) -> p (k c) n", c=4)
            for c in range(NCH):
                if c >= 4:
                    sp.wait_ge(s["second_add"], c - 3)
                for k in range(K):
                    sp.dma_start(ybuf[:, (c % 4) * 2 + k, :].rearrange("p (n d) -> p n d", d=D),
                                 y_tiles[k][:, c * CH:(c + 1) * CH, :]).then_inc(y_in[c % 4], 16)
                if c >= 2:
                    sp.wait_ge(s["second_add"], c - 1)
                    sp.dma_start(out_tiles[:, (c - 2) * CH:(c - 1) * CH, :],
                                 X[:, (c - 2) * CH:(c - 1) * CH, :]).then_inc(s["stored"], 16)
            for c in range(NCH - 2, NCH):
                sp.wait_ge(s["second_add"], c + 1)
                sp.dma_start(out_tiles[:, c * CH:(c + 1) * CH, :],
                             X[:, c * CH:(c + 1) * CH, :]).then_inc(s["stored"], 16)
            sp.wait_ge(s["stored"], 16 * NCH)

        @block.gpsimd
        def _(pool):
            pool.memset(ident[:], 0.0)
            pool.memset(tri[:], 0.0)
            pool.memset(ones[:], 1.0)
            pool.memset(eps_t[:], EPS)
            pool.memset(pad_rows[:, 0:D + 1], 0.0)
            pool.memset(pad_rows[:, D + 1:D + 2].bitcast(I32), SKIP)
            pool.memset(upto[:], 0.0)
            pool.memset(weigh[:], 1.0)
            pool.memset(rows[:], 0.0).then_inc(s["ident_zero"], 1)
            pool.wait_ge(s["ident_zero"], 1)
            pool.affine_select(out=ident[:], in_=ident[:], compare_op=ALU.not_equal, fill=1.0, base=0,
                               pattern=[[-1, P]], channel_multiplier=1)
            pool.affine_select(out=tri[:], in_=tri[:], compare_op=ALU.is_ge, fill=1.0, base=0,
                               pattern=[[-1, P]], channel_multiplier=1)
            pool.affine_select(out=upto[:], in_=upto[:], compare_op=ALU.is_gt, fill=1.0, base=0,
                               pattern=[[-1, E]], channel_multiplier=1)
            pool.iota(iota_e[:], pattern=[[1, E]], base=0, channel_multiplier=0,
                      allow_small_or_imprecise_dtypes=True)
            pool.iota(base0[:], pattern=[[STRIDE, E]], base=0, channel_multiplier=0,
                      allow_small_or_imprecise_dtypes=True)
            pool.iota(edge[:], pattern=[[0, 1]], base=0, channel_multiplier=P,
                      allow_small_or_imprecise_dtypes=True)
            pool.iota(tile_no[:], pattern=[[1, SLOTS]], base=0, channel_multiplier=0,
                      allow_small_or_imprecise_dtypes=True)
            pool.iota(row0[:], pattern=[[P, SLOTS]], base=0, channel_multiplier=0,
                      allow_small_or_imprecise_dtypes=True)
            pool.iota(dest[:], pattern=[[P, T], [TOK, K]], base=0, channel_multiplier=1,
                      allow_small_or_imprecise_dtypes=True).then_inc(s["consts_made"], 1)

            def weights_lo(g):
                ready(pool, "w1_hi", g)
                alone(pool)
                pool.tensor_tensor(W1lo[:, bass.ds(g * P, P)], W1s[:, bass.ds(g * P, P)],
                                   W1hi[:, bass.ds(g * P, P)].bitcast(F32), ALU.subtract).then_inc(s["w1_lo"], 1)
                ready(pool, "w2_hi", g)
                alone(pool)
                pool.tensor_tensor(W2hl[:, bass.ds(g, 1), 1, :].rearrange("p o d -> p (o d)"),
                                   W2s[:, bass.ds(g, 1), :].rearrange("p o d -> p (o d)"),
                                   W2hl[:, bass.ds(g, 1), 0, :].rearrange("p o d -> p (o d)").bitcast(F32),
                                   ALU.subtract).then_inc(s["w2_lo"], 1)

            def send_rows(g, b):
                if not isinstance(g, int) or g >= RB:
                    pool.wait_ge(rows_sent[b], (g - b) * 16)
                if not isinstance(g, int) or g >= 1:
                    pool.wait_ge(s["dest_moved"], g)
                alone(pool)
                pool.tensor_copy(rows[:, b, :, :, D + 1].bitcast(I32), dest[:]).then_inc(s["dest_ready"], 1)
                ready(pool, "dest_ready", g)
                alone(pool)
                pool.tensor_scalar(dest[:], dest[:], float(N), None, ALU.add).then_inc(s["dest_moved"], 1)
                ready(pool, "slots_ready", g)
                alone(pool)
                for t in range(T):
                    for k in range(K):
                        pool.indirect_dma_start(xs, bass.IndirectOffsetOnAxis(ap=slot[:, b, t, k:k + 1], axis=0),
                                                rows[:, b, t, k, :], None).then_inc(rows_sent[b], 16)

            pool.wait_ge(s["consts_made"], 1)

            def pool_step(i, j):
                if on(i, 0, G):
                    weights_lo(i)
                if on(i, RB, G):
                    send_rows(i - RB, j)

            steps_of(pool, 2 * RB, G, RB, RB, pool_step)

            def send_tile(i, b):
                ready(pool, "y_scaled", i)
                alone(pool)
                pool.indirect_dma_start(ytok, bass.IndirectOffsetOnAxis(ap=xt[:, b, D + 1:D + 2].bitcast(I32), axis=0),
                                        ys[:, b, :], None, bounds_check=SKIP - 1, oob_is_err=False
                                        ).then_inc(tile_out[b], 16)

            steps_of(pool, RING, SLOTS, RING, 0, send_tile)

        @block.tensor
        def _(pe):
            pe.wait_ge(s["consts_made"], 1)
            pe.wait_ge(s["small_in"], 64)
            nc.tensor.transpose(bank[0][:, 0:P], Wsb[:], ident[:]).then_inc(s["wt_ps"], 1)
            pe.wait_ge(s["wt_sb"], 1)
            nc.tensor.matmul(bank[1][:, 0:2], WT[:], a_sb[:], start=True, stop=True).then_inc(s["wa_ps"], 1)
            pe.wait_ge(s["wrep_ready"], 3)

            def transpose_xhat(g, b):
                ready(pe, "xhat_ready", g)
                freed(pe, "xhat_t_sb", g, 1)
                for t in range(T):
                    m = nc.tensor.transpose(bank[0][:, t * P:(t + 1) * P], xhat[:, b, t, :], ident[:])
                m.then_inc(s["xhat_t_ps"], 1)

            def project(g, b):
                ready(pe, "xhat_t_sb", g)
                freed(pe, "h_sb", g, 1)
                for t in range(T):
                    m = nc.tensor.matmul(bank[1][:, t * (D + 1):(t + 1) * (D + 1)], xhatT[:, b, t * P:(t + 1) * P],
                                         Waug[:], start=True, stop=True)
                m.then_inc(s["h_ps"], 1)
                ready(pe, "mask_ready", g)
                freed(pe, "relu_sb", g, 1)
                for t in range(T):
                    nc.tensor.matmul(bank[2][:, t * N:(t + 1) * N], wa2[:], xhatT[:, b, :], start=True, stop=False)
                    m = nc.tensor.matmul(bank[2][:, t * N:(t + 1) * N], ident16[:], mask[:, b, t, :],
                                         start=False, stop=True)
                m.then_inc(s["dst_ps"], 1)

            def transpose_p(g, b):
                ready(pe, "p_ready", g)
                freed(pe, "p_t_sb", g, 1)
                for j in range(T):
                    for t in range(T):
                        m = nc.tensor.transpose(bank[3][:, j * N + t * P:j * N + (t + 1) * P],
                                                p_sb[:, b, t, j * P:(j + 1) * P], ident[:])
                m.then_inc(s["p_t_ps"], 1)

            def attend(g, b):
                ready(pe, "p_t_sb", g)
                freed(pe, "x1_ready", g, 1)
                for t in range(T):
                    for j in range(T):
                        m = nc.tensor.matmul(bank[4][:, t * D:(t + 1) * D], pT[:, b, j, t * P:(t + 1) * P],
                                             h_sb[:, b, j, 0:D], start=(j == 0), stop=(j == T - 1))
                m.then_inc(s["attn_ps"], 1)

            def transpose_xn(g, b, rb):
                ready(pe, "rows_ready", g)
                freed(pe, "xn_t_sb", g, 1)
                for t in range(T):
                    m = nc.tensor.transpose(bank[5][:, t * P:(t + 1) * P], rows[:, rb, t, 0, 0:D], ident[:])
                m.then_inc(s["xn_t_ps"], 1)

            def gate(g, b):
                ready(pe, "xn_t_sb", g)
                freed(pe, "logits_sb", g, 1)
                for t in range(T):
                    m = nc.tensor.matmul(bank[6][:, t * E:(t + 1) * E], xnT[:, b, t * P:(t + 1) * P], Wg_sb[:],
                                         start=True, stop=True)
                m.then_inc(s["logits_ps"], 1)

            def count(g, b):
                ready(pe, "sel_ready", g)
                freed(pe, "base_ready", g, 1)
                c = bank[7]
                nc.tensor.matmul(c[:, 0:E], tri[:], sel[:, b, 0, :], start=True, stop=True)
                nc.tensor.matmul(c[:, E:2 * E], tri[:], sel[:, b, 1, :], start=True, stop=False)
                nc.tensor.matmul(c[:, E:2 * E], ones[:], sel[:, b, 0, :], start=False, stop=True)
                nc.tensor.matmul(c[:, 2 * E:3 * E], ones[:], sel[:, b, 0, :], start=True, stop=False)
                nc.tensor.matmul(c[:, 2 * E:3 * E], ones[:], sel[:, b, 1, :], start=False, stop=True
                                 ).then_inc(s["count_ps"], 1)

            def first_layer(i, j):
                b = j % 2
                if on(i, 2, G):
                    transpose_xhat(i - 2, b)
                if on(i, 4, G):
                    transpose_p(i - 4, b)
                if on(i, 6, G):
                    transpose_xn(i - 6, b, (j - 6) % RB)
                if on(i, 4, G):
                    attend(i - 4, b)
                if on(i, 2, G):
                    project(i - 2, b)
                if on(i, 6, G):
                    gate(i - 6, b)
                if on(i, 7, G):
                    count(i - 7, 1 - b)

            steps_of(pe, FIRST, G, RB, LAST, first_layer)

            pe.wait_ge(s["over_ready"], 1)
            nc.tensor.matmul(bank[7][0:E, 0:1], over[:], ones[:, 0:1], start=True, stop=True).then_inc(s["ntile_ps"], 1)
            pe.wait_ge(s["ntile_ready"], 1)
            nc.tensor.matmul(bank[6][0:E, 0:1], upto[:], ntile[:], start=True, stop=True).then_inc(s["cumend_ps"], 1)
            pe.wait_ge(s["weigh_ready"], 1)
            pe.wait_ge(s["past_ready"], 1)
            nc.tensor.matmul(bank[5][0:1, 0:SLOTS], weigh[:, 0:1], past[:], start=True, stop=True)
            nc.tensor.matmul(bank[5][0:1, SLOTS:2 * SLOTS], weigh[:, 1:2], past[:], start=True, stop=True
                             ).then_inc(s["sums_ps"], 1)
            pe.wait_ge(s["tab_ready"], 2)
            pe.wait_ge(s["w1_lo"], G)
            pe.wait_ge(s["w2_lo"], G)

            def turn_x(i, b, r):
                pe.wait_ge(tile_in[r], (i - r) * 2 + 16)
                freed(pe, "xt_lo", i)
                nc.tensor.transpose(bank[b][:, 0:P], xt[:, r, 0:D], ident[:]).then_inc(s["xt_ps"], 1)

            def up(i, b, e):
                ready(pe, "xt_lo", i)
                freed(pe, "biased", i)
                hi, lo = W1hi[:, bass.ds(e * H, H)], W1lo[:, bass.ds(e * H, H)]
                o = bank[2 + b]
                nc.tensor.matmul(o[:], xTh[:, b, :], hi, start=True, stop=False)
                nc.tensor.matmul(o[:], xTh[:, b, :], lo, start=False, stop=False)
                nc.tensor.matmul(o[:], xTl[:, b, :], hi, start=False, stop=True).then_inc(s["up_ps"], 1)

            def turn_g(i, b):
                ready(pe, "gelu_done", i)
                freed(pe, "gt_lo", i)
                for c in range(C):
                    m = nc.tensor.transpose(bank[4 + b][:, c * P:(c + 1) * P], g_sb[:, b, c * P:(c + 1) * P], ident[:])
                m.then_inc(s["gt_ps"], 1)

            def down(i, b, e):
                ready(pe, "gt_lo", i)
                freed(pe, "y_full", i)
                o = bank[6 + b]
                W2f = W2hl[:].rearrange("p b k d -> p (b k d)")
                for c in range(C):
                    nc.tensor.matmul(o[:, 0:2 * D], gTh[:, b, c * P:(c + 1) * P],
                                     W2f[:, bass.ds(e * (C * 2 * D) + c * 2 * D, 2 * D)],
                                     start=(c == 0), stop=False)
                    m = nc.tensor.matmul(o[:, 0:D], gTl[:, b, c * P:(c + 1) * P],
                                         W2f[:, bass.ds(e * (C * 2 * D) + c * 2 * D, D)],
                                         start=False, stop=(c == C - 1))
                m.then_inc(s["down_ps"], 1)

            def expert_step(i, j):
                b = j % 2
                if on(i, 0, SLOTS):
                    turn_x(i, b, j)
                if on(i, 1, SLOTS):
                    up(i - 1, 1 - b, experts[j - 1])
                if on(i, 2, SLOTS):
                    turn_g(i - 2, b)
                if on(i, 3, SLOTS):
                    down(i - 3, 1 - b, experts[j - 3])

            experts = {}
            steps_of(pe, RING, SLOTS, RING, 3, expert_step, read_experts(pe, experts, -3))

        @block.scalar
        def _(act):
            nc.scalar.preload_act_table_set("natural_log_exp_and_others")
            act.wait_ge(s["wt_ps"], 1)
            nc.scalar.activation(WT[:], bank[0][:, 0:P], ACT.Copy).then_inc(s["wt_sb"], 1)

            def roots(u, b, step):
                n = norms(u)
                if step == 0:
                    ready(act, "moments_ready", u)
                    nc.scalar.activation(root[:, b, 0, n, :], mean_var[:, b, n, :, 1], ACT.Ln, bias=eps_t[:, 0:1]
                                         ).then_inc(s["log_ready"], 1)
                else:
                    ready(act, "log_ready", u)
                    nc.scalar.activation(root[:, b, 1, n, :], root[:, b, 0, n, :], ACT.Exp, scale=-0.5
                                         ).then_inc(s["root_ready"], 1)

            def norm1(g, b):
                ready(act, "shift_ready", g)
                freed(act, "xhat_t_ps", g)
                for t in range(T):
                    m = nc.scalar.activation(xhat[:, b, t, :], X[:, bass.ds(g * T + t, 1), :].rearrange("p o d -> p (o d)"),
                                             ACT.Identity, bias=shift[:, b, t:t + 1], scale=root[:, b, 2, 0, t:t + 1])
                m.then_inc(s["xhat_ready"], 1)

            def take_scores(g, b, step):
                if step == 1:
                    ready(act, "h_sb", g)
                    freed(act, "p_ready", g)
                    for t in range(T):
                        m = nc.scalar.activation(relu_sb[:, b, t, :], bank[2][:, t * N:(t + 1) * N], ACT.Relu,
                                                 bias=h_sb[:, b, t, D:D + 1], scale=1.0 - SLOPE)
                    m.then_inc(s["relu_sb"], 1)
                    return
                ready(act, "h_ps", g)
                freed(act, "attn_ps", g)
                nc.scalar.activation(h_sb[:, b, :, :].rearrange("p t d -> p (t d)"), bank[1][:, 0:T * (D + 1)],
                                     ACT.Copy).then_inc(s["h_sb"], 1)
                ready(act, "dst_ps", g)
                freed(act, "e_max", g)
                nc.scalar.activation(dst_sb[:, b, :, :].rearrange("p t n -> p (t n)"), bank[2][:], ACT.Copy, scale=SLOPE).then_inc(s["dst_sb"], 1)

            def exps(g, b, t):
                if t == 0:
                    ready(act, "negmax_ready", g)
                    freed(act, "p_t_ps", g)
                    freed(act, "rinv_ready", g)
                m = nc.scalar.activation(p_sb[:, b, t, :], relu_sb[:, b, t, :], ACT.Exp, bias=nmax[:, b, t:t + 1],
                                         accum_out=psums[:, b, t:t + 1])
                if t == T - 1:
                    m.then_inc(s["p_ready"], 1)

            def copy_out(g, b, ps, dst, src, done, user):
                ready(act, ps, g)
                freed(act, user, g)
                nc.scalar.activation(dst, src, ACT.Copy).then_inc(s[done], 1)

            def gate_exp(g, b):
                ready(act, "gap_ready", g)
                nc.scalar.activation(gap[:, b, 1, :], gap[:, b, 0, :], ACT.Exp).then_inc(s["gap_exp"], 1)

            def split_weights(g, c):
                act.wait_ge(weights_in[c], (g - c) * 8 + 32)
                nc.scalar.activation(W1hi[:, bass.ds(g * P, P)], W1s[:, bass.ds(g * P, P)], ACT.Copy
                                     ).then_inc(s["w1_hi"], 1)
                nc.scalar.activation(W2hl[:, bass.ds(g, 1), 0, :].rearrange("p o d -> p (o d)"),
                                     W2s[:, bass.ds(g, 1), :].rearrange("p o d -> p (o d)"), ACT.Copy
                                     ).then_inc(s["w2_hi"], 1)

            def first_layer(i, j):
                b = j % 2
                c = 1 - b
                if on(i, 3, G):
                    take_scores(i - 3, c, 0)
                if on(i, 1, G + 4):
                    roots(i - 1, c, 0)
                if on(i, 1, G + 4):
                    roots(i - 1, c, 1)
                if on(i, 3, G):
                    take_scores(i - 3, c, 1)
                if on(i, 4, G):
                    copy_out(i - 4, b, "p_t_ps", pT[:, b, :, :].rearrange("p j n -> p (j n)"), bank[3][:],
                             "p_t_sb", "attn_ps")
                if on(i, 2, G):
                    copy_out(i - 2, b, "xhat_t_ps", xhatT[:, b, :], bank[0][:, 0:N], "xhat_t_sb", "dst_ps")
                if on(i, 6, G):
                    copy_out(i - 6, b, "xn_t_ps", xnT[:, b, :], bank[5][:, 0:N], "xn_t_sb", "logits_ps")
                if on(i, 7, G):
                    gate_exp(i - 7, c)
                if on(i, 3, G):
                    split_weights(i - 3, (j - 3) % C)
                if on(i, 1, G):
                    norm1(i - 1, c)
                if on(i, 3, G):
                    exps(i - 3, c, 0)
                    exps(i - 3, c, 1)

            steps_of(act, FIRST, G, C, LAST, first_layer)

            def expert_step(i, j):
                b = j % 2
                if on(i, 0, SLOTS):
                    ready(act, "xt_ps", i)
                    freed(act, "up_ps", i)
                    nc.scalar.activation(xTh[:, b, :], bank[b][:, 0:P], ACT.Copy).then_inc(s["xt_hi"], 1)
                if on(i, 5, SLOTS):
                    n, r = i - 5, (j - 5) % RING
                    ready(act, "y_full", n)
                    if isinstance(i, int):
                        if n >= RING:
                            act.wait_ge(tile_out[r], n // RING * 16)
                    else:
                        act.wait_ge(tile_out[r], (i - j) * 2 - (0 if j >= 5 else 16))
                    nc.scalar.activation(ys[:, r, :], yb[:, 1 - b, :], ACT.Copy, scale=xt[:, r, D:D + 1]
                                         ).then_inc(s["y_scaled"], 1)
                if on(i, 2, SLOTS):
                    ready(act, "gt_ps", i - 2)
                    freed(act, "down_ps", i - 2)
                    nc.scalar.activation(gTh[:, b, :], bank[4 + b][:], ACT.Copy).then_inc(s["gt_hi"], 1)
                if on(i, 1, SLOTS):
                    ready(act, "biased", i - 1)
                    freed(act, "gt_ps", i - 1)
                    nc.scalar.activation(g_sb[:, 1 - b, :], hb[:, 1 - b, :], ACT.Gelu).then_inc(s["gelu_done"], 1)

            steps_of(act, 2 * RING, SLOTS, RING, 5, expert_step)

        @block.vector
        def _(dve):
            dve.wait_ge(s["consts_made"], 1)
            dve.tensor_copy(ident16[:], ident[:]).then_inc(s["wrep_ready"], 1)
            dve.tensor_copy(base[:], base0[:]).then_inc(s["base_init"], 1)
            dve.wait_ge(s["wa_ps"], 1)
            dve.tensor_scalar(Waug[:, D:D + 1], bank[1][:, 0:1], 1.0 - SLOPE, None, ALU.mult).then_inc(s["wrep_ready"], 1)
            dve.tensor_copy(Waug[:, 0:D], Wsb[:]).then_inc(s["wa_sb"], 1)
            dve.tensor_copy(wa2[:], bank[1][:, 1:2].to_broadcast([P, P])).then_inc(s["wrep_ready"], 1)
            dve.wait_ge(s["wa_sb"], 1)
            dve.wait_ge(s["base_init"], 1)

            def xg(g, t):
                return X[:, bass.ds(g * T + t, 1), :].rearrange("p o d -> p (o d)")

            def stats(g, b, norm, done, t):
                m = dve.bn_stats(stat[:, b, norm, t, :], xg(g, t))
                if t == T - 1:
                    m.then_inc(s[done], 1)

            def moments(i, b):
                n = norms(i)
                if n.start == 0:
                    ready(dve, "ln1_stats", i)
                if n.stop == 2:
                    ready(dve, "ln2_stats", i - 4)
                alone(dve)
                for q in range(n.start, n.stop):
                    for t in range(T):
                        m = dve.bn_aggr(mean_var[:, b, q, t, :], stat[:, b, q, t, :])
                m.then_inc(s["moments_ready"], 1)

            def newton(u, b, step):
                n = norms(u)
                src, dst, num, op, done, wait = [
                    (mean_var[:, b, n, :, 1], 2, EPS, ALU.add, "newton1", "root_ready"),
                    (root[:, b, 2, n, :], 3, -0.5, ALU.mult, "newton2", "newton1"),
                    (root[:, b, 3, n, :], 2, 1.5, ALU.add, "rstd_ready", "newton2")][step]
                ready(dve, wait, u)
                dve.scalar_tensor_tensor(out=root[:, b, dst, n, :], in0=src, scalar=num, in1=root[:, b, 1, n, :],
                                         op0=op, op1=ALU.mult).then_inc(s[done], 1)

            def make_shift(g, b):
                ready(dve, "rstd_ready", g)
                dve.scalar_tensor_tensor(out=shift[:, b, :], in0=mean_var[:, b, 0, :, 0], scalar=-1.0,
                                         in1=root[:, b, 2, 0, :], op0=ALU.mult, op1=ALU.mult
                                         ).then_inc(s["shift_ready"], 1)

            def norm2(g, rb, t, u):
                if t == 0:
                    ready(dve, "rstd_ready", g + 4)
                    if not isinstance(g, int) or g >= RB:
                        dve.wait_ge(rows_sent[rb], (g - rb) * 16)
                m = dve.tensor_scalar(rows[:, rb, t, :, 0:D], X[:, bass.ds(g * T + t, 1), :].to_broadcast([P, K, D]),
                                      mean_var[:, u, 1, t, 0:1], root[:, u, 2, 1, t:t + 1], ALU.subtract, ALU.mult)
                if t == T - 1:
                    m.then_inc(s["rows_ready"], 1)

            def make_mask(g, b):
                dve.wait_ge(adj_in[b], (g - b) * 8 + 16)
                freed(dve, "dst_ps", g)
                dve.tensor_scalar(mask[:, b, :, :], adj_sb[:, b, :, :], 0.0, NEG / SLOPE, ALU.is_le, ALU.mult
                                  ).then_inc(s["mask_ready"], 1)

            def row_maxima(g, b):
                ready(dve, "relu_sb", g)
                ready(dve, "dst_sb", g)
                alone(dve)
                for t in range(T):
                    m = dve.tensor_tensor_reduce(relu_sb[:, b, t, :], relu_sb[:, b, t, :], dst_sb[:, b, t, :],
                                                 1.0, -3.0e38, ALU.add, ALU.max, emax[:, b, t:t + 1])
                m.then_inc(s["e_max"], 1)

            def negate_max(g, b):
                ready(dve, "e_max", g)
                dve.tensor_scalar(nmax[:, b, :], emax[:, b, :], -1.0, None, ALU.mult).then_inc(s["negmax_ready"], 1)

            def invert_sums(g, b):
                ready(dve, "p_ready", g)
                dve.reciprocal(rinv[:, b, :], psums[:, b, :]).then_inc(s["rinv_ready"], 1)

            def residual(g, b, t):
                if t == 0:
                    ready(dve, "rinv_ready", g)
                    ready(dve, "attn_ps", g)
                m = dve.scalar_tensor_tensor(out=xg(g, t), in0=bank[4][:, t * D:(t + 1) * D],
                                             scalar=rinv[:, b, t:t + 1], in1=xg(g, t), op0=ALU.mult, op1=ALU.add)
                if t == T - 1:
                    m.then_inc(s["x1_ready"], 1)

            def add_gate_bias(g, b):
                ready(dve, "logits_ps", g)
                dve.tensor_tensor(lg[:, b, :, :], bank[6][:, 0:T * E].rearrange("p (t e) -> p t e", t=T),
                                  bg_rep[:].rearrange("p (x e) -> p x e", x=1).to_broadcast([P, T, E]), ALU.add
                                  ).then_inc(s["logits_sb"], 1)

            def top_values(g, b):
                ready(dve, "logits_sb", g)
                alone(dve)
                for t in range(T):
                    m = dve.max(top[:, b, t, :], lg[:, b, t, :])
                m.then_inc(s["top_ready"], 1)

            def top_indices(g, b):
                ready(dve, "top_ready", g)
                alone(dve)
                dve.tensor_tensor(gap[:, b, 0, :], top[:, b, :, 1], top[:, b, :, 0], ALU.subtract
                                  ).then_inc(s["gap_ready"], 1)
                for t in range(T):
                    m = dve.max_index(topi[:, b, t, :], top[:, b, t, :], lg[:, b, t, :])
                m.then_inc(s["index_ready"], 1)

            def copy_picks(g, b):
                ready(dve, "index_ready", g)
                dve.tensor_copy(pick[:, b, :, :], topi[:, b, :, 0:K]).then_inc(s["picks_ready"], 1)

            def one_hot(g, b):
                ready(dve, "picks_ready", g)
                dve.tensor_tensor(hot[:, b, :, :, :].rearrange("p t k e -> p (t k) e"),
                                  iota_e[:].rearrange("p (x e) -> p x e", x=1).to_broadcast([P, T * K, E]),
                                  pick[:, b, :, :].rearrange("p t (k x) -> p (t k) x", x=1).to_broadcast([P, T * K, E]),
                                  ALU.is_equal).then_inc(s["onehot_ready"], 1)

            def select(g, b):
                ready(dve, "onehot_ready", g)
                freed(dve, "count_ps", g)
                dve.tensor_tensor(sel[:, b, :, :], hot[:, b, :, 0, :], hot[:, b, :, 1, :], ALU.add
                                  ).then_inc(s["sel_ready"], 1)

            def gates(g, b, rb, step):
                if step == 0:
                    ready(dve, "gap_exp", g)
                    dve.tensor_scalar(gap[:, b, 2, :], gap[:, b, 1, :], 1.0, None, ALU.add).then_inc(s["gate_den"], 1)
                if step == 1:
                    ready(dve, "gate_den", g)
                    dve.reciprocal(rows[:, rb, :, 0, D], gap[:, b, 2, :]).then_inc(s["gate_first"], 1)
                if step == 2:
                    ready(dve, "gate_first", g)
                    dve.tensor_tensor(rows[:, rb, :, 1, D], rows[:, rb, :, 0, D], gap[:, b, 1, :], ALU.mult
                                      ).then_inc(s["gates_ready"], 1)

            def place(g, b, rb, step):
                if step == 0:
                    ready(dve, "count_ps", g)
                    if not isinstance(g, int) or g >= 1:
                        dve.wait_ge(s["base_ready"], g)
                    dve.tensor_tensor(pos[:, b, :, :], bank[7][:, 0:T * E].rearrange("p (t e) -> p t e", t=T),
                                      base[:].rearrange("p (x e) -> p x e", x=1).to_broadcast([P, T, E]), ALU.add
                                      ).then_inc(s["pos_ready"], 1)
                if step == 1:
                    ready(dve, "pos_ready", g)
                    dve.tensor_tensor(base[:], bank[7][:, 2 * E:3 * E], base[:], ALU.add).then_inc(s["base_ready"], 1)
                    for t in range(T):
                        m = dve.tensor_tensor(posm[:, b, t, :, :], hot[:, b, t, :, :],
                                              pos[:, b, t:t + 1, :].to_broadcast([P, K, E]), ALU.mult)
                    m.then_inc(s["posmask_ready"], 1)
                if step == 2:
                    ready(dve, "posmask_ready", g)
                    ready(dve, "gates_ready", g)
                    with nc.allow_low_precision(reason="a sum of one row number and zeros, all whole"):
                        dve.tensor_reduce(slot[:, rb, :, :], posm[:, b, :, :, :], AX.X, ALU.add
                                          ).then_inc(s["slots_ready"], 1)

            def first_layer(i, j):
                b = j % 2
                c = 1 - b
                r6, r7, r8 = (j - 6) % RB, (j - 7) % RB, j % RB
                roots_on, norm_on, score_on, sum_on = on(i, 1, G + 4), on(i, 1, G), on(i, 3, G), on(i, 4, G)
                row_on, route_on, place_on = on(i, 6, G), on(i, 7, G), on(i, 8, G)
                if route_on:
                    add_gate_bias(i - 7, c)
                if row_on:
                    norm2(i - 6, r6, 0, b)
                if route_on:
                    top_values(i - 7, c)
                if row_on:
                    norm2(i - 6, r6, 1, b)
                if route_on:
                    top_indices(i - 7, c)
                if place_on:
                    place(i - 8, b, r8, 0)
                if roots_on:
                    newton(i - 1, c, 0)
                if route_on:
                    copy_picks(i - 7, c)
                if place_on:
                    place(i - 8, b, r8, 1)
                if roots_on:
                    newton(i - 1, c, 1)
                if route_on:
                    one_hot(i - 7, c)
                if roots_on:
                    newton(i - 1, c, 2)
                if route_on:
                    select(i - 7, c)
                if place_on:
                    place(i - 8, b, r8, 2)
                if norm_on:
                    make_shift(i - 1, c)
                if score_on:
                    row_maxima(i - 3, c)
                if on(i, 0, G):
                    dve.wait_ge(x_in[b], (i - b) * 8 + 16)
                    alone(dve)
                    stats(i, b, 0, "ln1_stats", 0)
                if score_on:
                    negate_max(i - 3, c)
                if on(i, 0, G):
                    stats(i, b, 0, "ln1_stats", 1)
                if route_on:
                    gates(i - 7, c, r7, 0)
                if sum_on:
                    invert_sums(i - 4, b)
                if route_on:
                    gates(i - 7, c, r7, 1)
                if sum_on:
                    residual(i - 4, b, 0)
                if route_on:
                    gates(i - 7, c, r7, 2)
                if sum_on:
                    residual(i - 4, b, 1)
                if norm_on:
                    make_mask(i - 1, c)
                if sum_on:
                    ready(dve, "x1_ready", i - 4)
                    alone(dve)
                    stats(i - 4, b, 1, "ln2_stats", 0)
                    stats(i - 4, b, 1, "ln2_stats", 1)
                if on(i, 0, G + 4):
                    moments(i, b)

            steps_of(dve, FIRST, G, RB, LAST, first_layer)

            dve.wait_ge(s["base_ready"], G)
            dve.tensor_copy(base_i[:], base[0:1, :]).then_inc(s["ends_ready"], 1)
            dve.scalar_tensor_tensor(out=over[:], in0=base[:], scalar=edge[:, 0:1], in1=base0[:],
                                     op0=ALU.subtract, op1=ALU.is_gt).then_inc(s["over_ready"], 1)
            dve.wait_ge(s["ntile_ps"], 1)
            dve.tensor_copy(ntile[:], bank[7][0:E, 0:1]).then_inc(s["ntile_ready"], 1)
            dve.tensor_scalar(weigh[:, 1:2], bank[7][0:E, 0:1], -float(P), float(STRIDE), ALU.mult, ALU.add
                              ).then_inc(s["weigh_ready"], 1)
            dve.wait_ge(s["cumend_ps"], 1)
            dve.tensor_copy(cumend[:], bank[6][0:E, 0:1]).then_inc(s["cumend_ready"], 1)
            dve.wait_ge(s["cumend_ready"], 1)
            dve.tensor_scalar(past[:], tile_no[:], cumend[:, 0:1], None, ALU.is_ge).then_inc(s["past_ready"], 1)
            dve.wait_ge(s["sums_ps"], 1)
            dve.tensor_scalar(eid_i[:, 0:SLOTS], bank[5][0:1, 0:SLOTS], float(E - 1), None, ALU.min
                              ).then_inc(s["tab_ready"], 1)
            dve.tensor_tensor(row_i[:, 0:SLOTS], bank[5][0:1, SLOTS:2 * SLOTS], row0[:], ALU.add
                              ).then_inc(s["tab_ready"], 1)
            dve.wait_ge(s["tab_ready"], 2)

            dve.wait_ge(s["biases_in"], 32)

            def expert_step(i, j):
                b = j % 2
                if on(i, 3, SLOTS):
                    ready(dve, "gt_hi", i - 3)
                    dve.tensor_tensor(gTl[:, 1 - b, :], bank[5 - b][:], gTh[:, 1 - b, :].bitcast(F32), ALU.subtract
                                      ).then_inc(s["gt_lo"], 1)
                if on(i, 0, SLOTS):
                    ready(dve, "xt_hi", i)
                    dve.tensor_tensor(xTl[:, b, :], bank[b][:, 0:P], xTh[:, b, :].bitcast(F32), ALU.subtract
                                      ).then_inc(s["xt_lo"], 1)
                if on(i, 1, SLOTS):
                    n, q, e = i - 1, 1 - b, experts[j - 1]
                    ready(dve, "up_ps", n)
                    freed(dve, "gelu_done", n)
                    dve.tensor_tensor(hb[:, q, :], bank[2 + q][:],
                                      b1_rep[:, bass.ds(e, 1), :].rearrange("p o h -> p (o h)"), ALU.add
                                      ).then_inc(s["biased"], 1)
                if on(i, 4, SLOTS):
                    n, e = i - 4, experts[j - 4]
                    ready(dve, "down_ps", n)
                    dve.tensor_tensor(ya[:, b, :], bank[6 + b][:, 0:D],
                                      b2_rep[:, bass.ds(e, 1), :].rearrange("p o h -> p (o h)"), ALU.add
                                      ).then_inc(s["y_half"], 1)
                    ready(dve, "y_half", n)
                    freed(dve, "y_scaled", n)
                    dve.tensor_tensor(yb[:, b, :], bank[6 + b][:, D:2 * D], ya[:, b, :], ALU.add
                                      ).then_inc(s["y_full"], 1)

            experts = {}
            steps_of(dve, RING, SLOTS, RING, 4, expert_step, read_experts(dve, experts, -4))

            ybuf = Wstage[:].rearrange("p k (c n) -> p (k c) n", c=4)
            for c in range(NCH):
                xc = X[:, c * CH:(c + 1) * CH, :].rearrange("p n d -> p (n d)")
                dve.wait_ge(y_in[c % 4], 32 * (c // 4 + 1))
                dve.tensor_tensor(xc, xc, ybuf[:, (c % 4) * 2, :], ALU.add).then_inc(s["first_add"], 1)
                dve.wait_ge(s["first_add"], c + 1)
                dve.tensor_tensor(xc, xc, ybuf[:, (c % 4) * 2 + 1, :], ALU.add).then_inc(s["second_add"], 1)


_INS = ['x', 'adj', 'L0_gnn_W', 'L0_gnn_a', 'L0_ffn_Wg', 'L0_ffn_bg', 'L0_ffn_W1', 'L0_ffn_b1', 'L0_ffn_W2', 'L0_ffn_b2']


def kernel(**inputs):
    import numpy as _np
    import concourse.bacc as _bacc
    from concourse import mybir as _mybir
    from concourse.bass_utils import run_bass_kernel_spmd as _run

    nc = _bacc.Bacc("TRN2", target_bir_lowering=False, num_devices=1)
    arrays, args = {}, []
    for name in _INS:
        v = _np.ascontiguousarray(inputs[name])
        arrays[f"in_{name}_dram"] = v
        args.append(nc.dram_tensor(f"in_{name}_dram", v.shape, _mybir.dt.from_np(v.dtype), kind="ExternalInput").ap())
    args.append(nc.dram_tensor("out_dram", (G, N, D), _mybir.dt.float32, kind="ExternalOutput").ap())
    build(nc, *args)
    r = _run(nc, [arrays], core_ids=[0])
    return r.results[0]["out_dram"]
```
